# Optimizing a Trainium2 kernel written in Bass

```python
import numpy as np
import jax
import jax.numpy as jnp

def _softmax(x, axis=-1):
    return jax.nn.softmax(x, axis=axis)

def _gelu(x):
    return jax.nn.gelu(x, approximate=True)

def _silu(x):
    return jax.nn.silu(x)

def _sigmoid(x):
    return jax.nn.sigmoid(x)

def _layernorm(x, axis=-1, eps=1e-05):
    m = jnp.mean(x, axis=axis, keepdims=True)
    v = jnp.var(x, axis=axis, keepdims=True)
    return (x - m) / jnp.sqrt(v + eps)

def _scatter_add(tgt, idx, src, axis=0):
    return tgt.at[idx].add(src)

def _segment_sum(src, seg, n):
    return jax.ops.segment_sum(src, seg, n)
kernel_name = 'mk_prb_d1_jaxref_r8_591e25'

def setup_inputs(seed: int=0):
    np.random.seed(seed)
    _w = jnp.asarray

    def _L0_attn_setup():
        import jax, jax.numpy as jnp
        import numpy as np
        EPS = 1e-05

        def xpos_rotate(x, offset=0, conjugate=False):
            b, s, h, dh = x.shape
            expoent = jnp.arange(0, dh, 2, dtype=jnp.float32) / dh
            angle = 10.0 ** (-4.0 * expoent)
            if conjugate:
                angle = -angle
            pos = jnp.arange(offset, s + offset, dtype=jnp.float32)
            nangle = pos[:, None] * angle[None, :]
            sin = jnp.sin(nangle)[None, :, None, :]
            cos = jnp.cos(nangle)[None, :, None, :]
            x0 = x[..., 0::2]
            x1 = x[..., 1::2]
            rot = jnp.stack([x0 * cos - x1 * sin, x0 * sin + x1 * cos], axis=-1)
            return rot.reshape(b, s, h, dh)

        def decay_mask(nseq, scale):
            idx = jnp.arange(nseq)
            diff = idx[:, None] - idx[None, :]
            mask = (diff >= 0).astype(scale.dtype)
            diff_c = jnp.maximum(diff, 0).astype(scale.dtype)
            logd = diff_c[None, :, :] * jnp.log(scale)[:, None, None]
            return jnp.exp(logd) * mask[None, :, :]

        def group_norm(R, gamma, beta, nheads):
            b, s, d = R.shape
            dh = d // nheads
            Rg = R.reshape(b, s, nheads, dh)
            mu = jnp.mean(Rg, axis=-1, keepdims=True)
            var = jnp.var(Rg, axis=-1, keepdims=True)
            Rn = (Rg - mu) * jax.lax.rsqrt(var + EPS)
            Rn = Rn * gamma.reshape(1, 1, nheads, dh) + beta.reshape(1, 1, nheads, dh)
            return Rn.reshape(b, s, d)
        key = jax.random.key(seed)
        ks = jax.random.split(key, 7)
        b, s, d, h = (2, 256, 128, 16)
        dh = d // h
        x = jax.random.normal(ks[0], (b, s, d), dtype=jnp.float32)
        std_qkv = float(np.sqrt(2.0 / (dh + d)))
        std_o = float(np.sqrt(2.0 / (d + d)))
        WQ = jax.random.normal(ks[1], (h, dh, d), dtype=jnp.float32) * std_qkv
        WK = jax.random.normal(ks[2], (h, dh, d), dtype=jnp.float32) * std_qkv
        WV = jax.random.normal(ks[3], (h, dh, d), dtype=jnp.float32) * std_qkv
        WO = jax.random.normal(ks[4], (d, d), dtype=jnp.float32) * std_o
        gamma = jnp.ones((d,), dtype=jnp.float32)
        beta = jnp.zeros((d,), dtype=jnp.float32)
        return {'x': x, 'WQ': WQ, 'WK': WK, 'WV': WV, 'WO': WO, 'gamma': gamma, 'beta': beta}
    _L0_attn_in = _L0_attn_setup()

    def _L0_ffn_setup():
        import jax, jax.numpy as jnp
        import numpy as np
        D_MODEL = 128
        D_HIDDEN = 512
        NUM_EXPERT = 8
        TOP_K = 2
        B, N = (1, 1024)

        def _expert_mlp(x, W1, b1, W2, b2, W3, b3):
            h = jax.nn.gelu(jnp.einsum('bnd,dh->bnh', x, W1) + b1, approximate=False)
            h = jax.nn.gelu(jnp.einsum('bnh,hk->bnk', h, W2) + b2, approximate=False)
            return jnp.einsum('bnh,hd->bnd', h, W3) + b3
        key = jax.random.key(seed)
        ks = jax.random.split(key, 8)
        s1 = 1.0 / np.sqrt(D_MODEL)
        s2 = 1.0 / np.sqrt(D_HIDDEN)
        return {'x': jax.random.normal(ks[0], (B, N, D_MODEL), jnp.float32), 'expert_tokens': jax.random.normal(ks[1], (NUM_EXPERT, D_MODEL), jnp.float32), 'W1': jax.random.normal(ks[2], (NUM_EXPERT, D_MODEL, D_HIDDEN), jnp.float32) * s1, 'b1': jnp.zeros((NUM_EXPERT, D_HIDDEN), jnp.float32), 'W2': jax.random.normal(ks[3], (NUM_EXPERT, D_HIDDEN, D_HIDDEN), jnp.float32) * s2, 'b2': jnp.zeros((NUM_EXPERT, D_HIDDEN), jnp.float32), 'W3': jax.random.normal(ks[4], (NUM_EXPERT, D_HIDDEN, D_MODEL), jnp.float32) * s2, 'b3': jnp.zeros((NUM_EXPERT, D_MODEL), jnp.float32)}
    _L0_ffn_in = _L0_ffn_setup()
    _d = {'L0_attn_x': _L0_attn_in['x'], 'L0_attn_WQ': _L0_attn_in['WQ'], 'L0_attn_WK': _L0_attn_in['WK'], 'L0_attn_WV': _L0_attn_in['WV'], 'L0_attn_WO': _L0_attn_in['WO'], 'L0_attn_gamma': _L0_attn_in['gamma'], 'L0_attn_beta': _L0_attn_in['beta'], 'L0_ffn_expert_tokens': _L0_ffn_in['expert_tokens'], 'L0_ffn_W1': _L0_ffn_in['W1'], 'L0_ffn_b1': _L0_ffn_in['b1'], 'L0_ffn_W2': _L0_ffn_in['W2'], 'L0_ffn_b2': _L0_ffn_in['b2'], 'L0_ffn_W3': _L0_ffn_in['W3'], 'L0_ffn_b3': _L0_ffn_in['b3']}
    _x0 = _d['L0_attn_x']
    _d['L0_attn_x'] = jax.random.normal(jax.random.fold_in(jax.random.key(seed), 1), (8, 256, 128), dtype=_x0.dtype)
    del _x0
    return _d

def reference(L0_attn_x, L0_attn_WQ, L0_attn_WK, L0_attn_WV, L0_attn_WO, L0_attn_gamma, L0_attn_beta, L0_ffn_expert_tokens, L0_ffn_W1, L0_ffn_b1, L0_ffn_W2, L0_ffn_b2, L0_ffn_W3, L0_ffn_b3):

    def _L0_attn_ref(x, WQ, WK, WV, WO, gamma, beta):
        import jax, jax.numpy as jnp
        import numpy as np
        EPS = 1e-05

        def xpos_rotate(x, offset=0, conjugate=False):
            b, s, h, dh = x.shape
            expoent = jnp.arange(0, dh, 2, dtype=jnp.float32) / dh
            angle = 10.0 ** (-4.0 * expoent)
            if conjugate:
                angle = -angle
            pos = jnp.arange(offset, s + offset, dtype=jnp.float32)
            nangle = pos[:, None] * angle[None, :]
            sin = jnp.sin(nangle)[None, :, None, :]
            cos = jnp.cos(nangle)[None, :, None, :]
            x0 = x[..., 0::2]
            x1 = x[..., 1::2]
            rot = jnp.stack([x0 * cos - x1 * sin, x0 * sin + x1 * cos], axis=-1)
            return rot.reshape(b, s, h, dh)

        def decay_mask(nseq, scale):
            idx = jnp.arange(nseq)
            diff = idx[:, None] - idx[None, :]
            mask = (diff >= 0).astype(scale.dtype)
            diff_c = jnp.maximum(diff, 0).astype(scale.dtype)
            logd = diff_c[None, :, :] * jnp.log(scale)[:, None, None]
            return jnp.exp(logd) * mask[None, :, :]

        def group_norm(R, gamma, beta, nheads):
            b, s, d = R.shape
            dh = d // nheads
            Rg = R.reshape(b, s, nheads, dh)
            mu = jnp.mean(Rg, axis=-1, keepdims=True)
            var = jnp.var(Rg, axis=-1, keepdims=True)
            Rn = (Rg - mu) * jax.lax.rsqrt(var + EPS)
            Rn = Rn * gamma.reshape(1, 1, nheads, dh) + beta.reshape(1, 1, nheads, dh)
            return Rn.reshape(b, s, d)
        b, s, d = x.shape
        h, dh, _ = WQ.shape
        Q = jnp.einsum('bsd,hud->bshu', x, WQ)
        K = jnp.einsum('bsd,hud->bshu', x, WK)
        V = jnp.einsum('bsd,hud->bshu', x, WV)
        Q = xpos_rotate(Q)
        K = xpos_rotate(K)
        QK = jnp.einsum('bihd,bjhd->bhij', Q, K)
        scale = 1.0 - 2.0 ** (-5.0 - jnp.arange(h, dtype=jnp.float32))
        D = decay_mask(s, scale)
        QKD = QK * D[None]
        R = jnp.einsum('bhij,bjhd->bihd', QKD, V)
        R = R.reshape(b, s, d)
        R = group_norm(R, gamma, beta, h)
        y = R @ WO
        return y

    def _L0_ffn_ref(x, expert_tokens, W1, b1, W2, b2, W3, b3):
        import jax, jax.numpy as jnp
        import numpy as np
        D_MODEL = 128
        D_HIDDEN = 512
        NUM_EXPERT = 8
        TOP_K = 2
        B, N = (1, 1024)

        def _expert_mlp(x, W1, b1, W2, b2, W3, b3):
            h = jax.nn.gelu(jnp.einsum('bnd,dh->bnh', x, W1) + b1, approximate=False)
            h = jax.nn.gelu(jnp.einsum('bnh,hk->bnk', h, W2) + b2, approximate=False)
            return jnp.einsum('bnh,hd->bnd', h, W3) + b3
        scores = jnp.einsum('bnd,ed->bne', x, expert_tokens)
        _, topk_idx = jax.lax.top_k(scores, TOP_K)
        outputs = jnp.zeros_like(x)
        num_expert = W1.shape[0]
        for i in range(num_expert):
            w = jnp.mean((topk_idx == i).astype(x.dtype), axis=-1, keepdims=True)
            y = _expert_mlp(x, W1[i], b1[i], W2[i], b2[i], W3[i], b3[i])
            outputs = outputs + y * w
        return outputs
    x = L0_attn_x
    xn = _layernorm(x, axis=-1)
    x = x + _L0_attn_ref(xn, L0_attn_WQ, L0_attn_WK, L0_attn_WV, L0_attn_WO, L0_attn_gamma, L0_attn_beta) + _L0_ffn_ref(xn, L0_ffn_expert_tokens, L0_ffn_W1, L0_ffn_b1, L0_ffn_W2, L0_ffn_b2, L0_ffn_W3, L0_ffn_b3)
    return x

_drawn_inputs = setup_inputs


def setup_inputs(seed=0):
    import zlib

    import numpy as np

    out = dict(_drawn_inputs(seed))
    spreads = {'L0_attn_gamma': (1.0, 0.2),
     'L0_attn_beta': (0.0, 0.1),
     'L0_ffn_b1': (0.0, 0.392),
     'L0_ffn_b2': (0.0, 0.1),
     'L0_ffn_b3': (0.0, 0.1)}
    factors = {}
    for name, (base, spread) in spreads.items():
        noise = np.random.default_rng([zlib.crc32(name.encode()), seed]).standard_normal(out[name].shape)
        drawn = base * np.exp(spread * noise) if base else spread * noise
        out[name] = jnp.asarray(drawn.astype(out[name].dtype))
    for name, factor in factors.items():
        out[name] = (out[name] * factor).astype(out[name].dtype)
    return out
```

```python
import numpy as np
import concourse.bass as bass
from concourse import mybir

F32 = mybir.dt.float32
F32R = mybir.dt.float32r
BF16 = mybir.dt.bfloat16
I32 = mybir.dt.int32
U32 = mybir.dt.uint32
ALU = mybir.AluOpType
ACT = mybir.ActivationFunctionType
AX = mybir.AxisListType

NTOK, D, HID, NEXP = 2048, 128, 512, 8
NTT = NTOK // 128
NB, SEQ, NHEAD = 8, 256, 16
NT = 39
NTP = 40
LATE = 2

C_ID, C_MASK, C_BLK, C_CEN, C_AVG = 0, 128, 256, 384, 512
C_TAB = 640
C_HM = 1664
C_P, C_PM = 1668, 1669
C_IT = 1670
C_K = 1710
C_L = 1726
C_N = 1790
B_IO, B_TRI, B_ONE, B_LM = 0, 128, 256, 384
B_N = 448


def constants():
    c = np.zeros((128, C_N), np.float32)
    p = np.arange(128)
    c[:, C_ID:C_ID + 128] = np.eye(128)
    c[:, C_MASK:C_MASK + 128] = p[None, :] >= p[:, None]
    same = (p[:, None] // 8) == (p[None, :] // 8)
    c[:, C_BLK:C_BLK + 128] = same
    c[:, C_CEN:C_CEN + 128] = np.eye(128) - same / 8.0
    c[:, C_AVG:C_AVG + 128] = same / 8.0
    ex = np.arange(0, 8, 2, dtype=np.float32) / np.float32(8)
    angle = np.power(np.float32(10.0), np.float32(-4.0) * ex).astype(np.float32)
    pos = np.arange(SEQ, dtype=np.float32)
    ang = (pos[None, :] * angle[(p % 8) // 2][:, None]).astype(np.float32).astype(np.float64)
    sgn = np.where(p % 2 == 0, -1.0, 1.0)[:, None]
    g = (1.0 - 2.0 ** (-5.0 - (p // 8)))[:, None]
    up, down = g ** pos[None, :], g ** -pos[None, :].astype(np.float64)
    for n, t in enumerate((np.cos(ang) * up, np.sin(ang) * sgn * up, np.cos(ang) * down, np.sin(ang) * sgn * down)):
        c[:, C_TAB + 256 * n:C_TAB + 256 * (n + 1)] = t
    for m in range(4):
        c[:, C_HM + m] = ((p // 8) % 4) == m
    c[:, C_P] = p
    c[:, C_PM] = p % 32
    c[:, C_IT:C_IT + NTP] = np.arange(NTP)
    c[:, C_K:C_K + 16] = 128 * np.arange(16)
    e = np.arange(8)
    c[:, C_L:C_L + 64] = (e[None, :] < e[:, None]).reshape(1, 64)
    b = np.zeros((128, B_N), np.float32)
    b[:, B_IO:B_IO + 128] = p[None, :]
    b[:, B_TRI:B_TRI + 128] = p[:, None] < p[None, :]
    b[:, B_ONE:B_ONE + 128] = 1
    b[:, B_LM:B_LM + 64] = (e[None, :] < e[:, None]).reshape(1, 64)
    return c, b


class Queue:

    def __init__(self, sem):
        self.sem, self.n, self.ops = sem, 0, []

    def __call__(self, fn, *needs, sig=True):
        self.ops.append((fn, [x for x in needs if x is not None], sig))
        if sig:
            self.n += 1
            return (self.sem, self.n)

    def dma(self, fn, done, *needs):
        self.ops.append((fn, [x for x in needs if x is not None], done.sem))
        done.n += 16
        return (done.sem, done.n)

    def emit(self, eng):
        seen = {}
        for fn, needs, sig in self.ops:
            for sem, value in needs:
                if seen.get(sem.name, 0) < value:
                    eng.wait_ge(sem, value)
                    seen[sem.name] = value
            ins = fn()
            if sig is True:
                ins.then_inc(self.sem, 1)
            elif sig is not False:
                ins.then_inc(sig, 16)


class DmaSem:
    def __init__(self, sem):
        self.sem, self.n = sem, 0


def moe_retention_kernel(nc, x, wqkv, wvo, gb, etokT, w1, w2, w3, bias, cf, cb, out):
    def at(name, cols, dt, off, parts=128):
        return nc.alloc_sbuf_tensor_at(name, [parts, cols], dt, offset=off)

    R0 = 16512
    W2H, W2L = R0, R0 + 65536
    W1H, W1L, W3O = R0 + 131072, R0 + 147456, R0 + 163840
    BO = R0 + 180224
    F0 = BO + 4608
    w2h = at("w2h", 8 * 2048, F32R, W2H)
    w2l = at("w2l", 8 * 2048, F32R, W2L)
    w1h = at("w1h", 8 * 512, F32R, W1H)
    w1l = at("w1l", 8 * 512, F32R, W1L)
    w3s = at("w3s", 8 * 512, F32, W3O)
    ball = at("ball", 1152, F32R, BO)
    o = F0
    ident = at("ident", 128, F32, o); o += 512
    gidx = at("gidx", NTP, U32, o); o += 160
    sidx = at("sidx", NTP, U32, o); o += 160
    ex = at("ex", NTP, F32, o); o += 160
    exi = at("exi", NTP, I32, o); o += 160
    pm = at("pm", 1, F32, o); o += 32
    stg = [at(f"stg{i}", 512, F32, o + 2048 * i) for i in range(4)]; o += 8192
    G0 = o
    xg = [at(f"xg{i}", 128, F32, (o if i < 2 else G0 - 4096 - 1024) + 512 * i) for i in range(4)]; o += 1024
    xh = [at(f"xh{i}", 128, F32R, o + 1024 * i) for i in range(2)]
    xl = [at(f"xl{i}", 128, F32R, o + 512 + 1024 * i) for i in range(2)]; o += 2048
    g1 = at("g1", 512, F32, o); o += 2048
    h1h = at("h1h", 512, F32R, o); o += 2048
    h1l = at("h1l", 512, F32R, o); o += 2048
    g2 = at("g2", 512, F32, o); o += 2048
    h2t = [at(f"h2t{i}", 512, F32, o + 2048 * i) for i in range(2)]; o += 4096
    ys = [at(f"ys{i}", 128, F32, o + 512 * i) for i in range(2)]; o += 1024
    sel = [at(f"sel{i}", 128, F32R, G0 - 8192 + 512 * i) for i in range(5)]
    assert o <= 229368
    o = G0
    cs = at("cs", 512, F32, o); o += 2048
    small = at("small", C_N - C_HM, F32, o); o += 512
    cbs = at("cbs", B_N, BF16, o); o += 896
    wq = at("wq", 512, F32, o); o += 2048
    wv = at("wv", 256, F32, o); o += 1024
    gbt = at("gbt", 2, F32, o); o += 32
    et = at("et", 8, F32, o); o += 32
    xr = at("xr", 256, F32, o); o += 1024
    vs = at("vs", 128, F32, o); o += 512
    rt = at("rt", 256, F32, o); o += 1024
    sq = at("sq", 256, F32, o); o += 1024
    rs = at("rs", 256, F32, o); o += 1024
    rn = at("rn", 256, F32, o); o += 1024
    ob = [at(f"ob{i}", 256, F32, o + 1024 * i) for i in range(2)]; o += 2048
    qr0 = at("qr0", 256, F32, o); o += 1024
    kr0 = at("kr0", 256, F32, o); o += 1024
    st = at("st", 96, F32, o); o += 384
    mv = at("mv", 32, F32, o); o += 128
    rstd = at("rstd", 16, F32, o); o += 64
    eps = at("eps", 1, F32, o); o += 32
    assert o <= 229368, o
    A0 = W2H + 49152
    xn = at("xn", 2048, F32, A0)
    xnt = at("xnt", 2048, F32, A0 + 8192)
    o = A0
    gt = at("gt", 1024, BF16, o); o += 2048
    eq = at("eq", 1024, BF16, o); o += 2048
    oh = [at(f"oh{i}", 128, BF16, A0 + 256 * i) for i in range(8)]
    bt = [at(f"bt{i}", 2 * NTP, BF16, A0 + 2048 + 160 * i) for i in range(8)]
    sc = at("sc", 128, F32, o); o += 512
    msk = at("msk", 128, BF16, o); o += 256
    s0 = at("s0", 128, F32, o); o += 512
    s1 = at("s1", 128, F32, o); o += 512
    cm = at("cm", 128, F32, o); o += 512
    ne = at("ne", 8, F32, o); o += 32
    ce = at("ce", 8, F32, o); o += 32
    be = at("be", 8, F32, o); o += 32
    dst = at("dst", 32, F32, o); o += 128
    dsi = at("dsi", 32, I32, o); o += 128
    dhi = at("dhi", 32, I32, o); o += 128
    dlo = at("dlo", 32, I32, o); o += 128
    dtf = at("dtf", 32, F32, o); o += 128
    dpf = at("dpf", 32, F32, o); o += 128
    tbh = at("tbh", 2 * NTP, F32, o); o += 320
    tbg = at("tbg", NTP, F32, o); o += 160
    tbe = at("tbe", NTP, F32, o); o += 160
    assert o <= A0 + 8192
    B0 = W2L + 49152
    pt = [at(f"pt{i}", 512, F32, B0 + 2048 * i) for i in range(3)]
    braw = at("braw", 1152, F32, B0)
    btmp = at("btmp", 1152, F32R, B0 + 4608)
    qx0 = at("qx0", 1024, F32, B0 + 6144)
    tmp = at("tmp", 1024, F32, B0 + 10240)
    kt = at("kt", 128, F32, B0 + 14336)
    smt = at("smt", 128, F32, B0 + 14848)
    kr1 = at("kr1", 256, F32, B0 + 15360)
    vm = [at(f"vm{i}", 512, F32, W1H + 12288 + 2048 * i) for i in range(2)]
    qx1 = at("qx1", 1024, F32, W1L + 12288)
    tab = at("tab", 1024, F32, W3O + 12288)
    qr, kr, qx = [qr0, qr0], [kr0, kr1], [qx0, qx1]
    ps = [nc.alloc_psum_tensor(f"ps{i}", [128, 512], F32) for i in range(8)]
    xnd = nc.dram_tensor("xnd", (NTOK, D), F32, kind="Internal").ap()

    cmask, cblk, ccen, cavg = (cs[:, 128 * i:128 * i + 128] for i in range(4))
    hm = lambda m: small[:, m:m + 1]
    pcol = small[:, C_P - C_HM:C_P - C_HM + 1]
    pmcol = small[:, C_PM - C_HM:C_PM - C_HM + 1]
    iot = small[:, C_IT - C_HM:C_IT - C_HM + NTP]
    k128 = small[:, C_K - C_HM:C_K - C_HM + 16]
    lm8 = small[:, C_L - C_HM:C_L - C_HM + 64]
    b_io, b_tri, b_one = (cbs[:, 128 * i:128 * i + 128] for i in range(3))
    b_lm = cbs[:, B_LM:B_LM + 64]

    S = lambda name: nc.alloc_semaphore(name)
    pe, act, dve, pool, sp = (Queue(S(f"q_{n}")) for n in ("pe", "act", "dve", "pool", "sp"))
    d_const, d_x, d_xn = DmaSem(S("d_const")), DmaSem(S("d_x")), DmaSem(S("d_xn"))
    d_bias, d_w3, d_base = DmaSem(S("d_bias")), DmaSem(S("d_w3")), DmaSem(S("d_base"))
    d_xr = DmaSem(S("d_xr"))
    d_stg = [DmaSem(S(f"d_stg{i}")) for i in range(4)]
    d_g = [DmaSem(S(f"d_g{i}")) for i in range(4)]
    d_s = DmaSem(S("d_s"))
    V, A, G, T = nc.vector, nc.scalar, nc.gpsimd, nc.tensor

    xt = x.rearrange("(t p) d -> p t d", p=128)
    xv = xn[:].rearrange("p (t d) -> p t d", d=128)
    d_x4 = [DmaSem(S(f"d_x{i}")) for i in range(4)]
    e_x = []
    for i in range(4):
        e_x.append(sp.dma(lambda i=i: nc.sync.dma_start(xv[:, 4 * i:4 * i + 4, :], xt[:, 4 * i:4 * i + 4, :]), d_x4[i]))
    for dst_, src_ in ((ident[:], cf[:, 0:128]), (cs[:], cf[:, 128:640]), (small[:], cf[:, C_HM:C_N]),
                       (tmp[:, 0:B_N], cb), (et[:], etokT), (wq[:], wqkv), (wv[:], wvo), (gbt[:], gb),
                       (tab[:], cf[:, C_TAB:C_TAB + 1024])):
        e_c = act.dma(lambda a=dst_, b=src_: nc.scalar.dma_start(a, b), d_const)
    e_z = dve(lambda: V.memset(braw[0:64, :], 0.0))
    act.dma(lambda: nc.scalar.dma_start(braw[0:8, :], bias), d_bias, e_z)
    e_b = act.dma(lambda: nc.scalar.dma_start(braw[32:40, :], bias), d_bias, e_z)
    e_w3 = act.dma(lambda: nc.scalar.dma_start(
        w3s[:].rearrange("p (e c k) -> p e c k", e=8, c=4)[:, 0:6].rearrange("p e c k -> p (e c) k"),
        w3[0:6].rearrange("e (c p) k -> p (e c) k", p=128)), d_w3)

    w2src = w2.rearrange("e (c p) k -> e c p k", p=128)
    pieces = []
    for e in range(8):
        for c in range(4):
            pieces.append((w2src[e, c], w2h[:, e * 2048 + c * 512:][:, 0:512], w2l[:, e * 2048 + c * 512:][:, 0:512]))
        pieces.append((w1[e], w1h[:, e * 512:(e + 1) * 512], w1l[:, e * 512:(e + 1) * 512]))
    last_lo = [None] * 4
    staged = [0]
    w_done = {}

    def stage(after=()):
        i = staged[0]
        staged[0] += 1
        src, hi, lo = pieces[i]
        b = i % 4
        ld = sp.dma(lambda: nc.sync.dma_start(stg[b][:], src), d_stg[b], last_lo[b])
        h = act(lambda: A.copy(hi, stg[b][:]), ld, *after)
        if i % 2 or i >= 30:
            last_lo[b] = dve(lambda: V.tensor_tensor(lo, stg[b][:], hi, ALU.subtract), h)
            w_done["v"] = last_lo[b]
        else:
            last_lo[b] = pool(lambda: G.tensor_tensor(lo, stg[b][:], hi, ALU.subtract), h)
            w_done["p"] = last_lo[b]

    e_eps = dve(lambda: V.memset(eps[:], 1e-5))
    for t in range(16):
        e = dve(lambda t=t: V.bn_stats(st[:, 6 * t:6 * t + 6], xn[:, 128 * t:128 * t + 128]), e_x[t // 4])
    for t in range(16):
        e = dve(lambda t=t: V.bn_aggr(mv[:, 2 * t:2 * t + 2], st[:, 6 * t:6 * t + 6]), e)
    mvv = mv[:].rearrange("p (t k) -> p t k", k=2)
    e = act(lambda: A.activation(rstd[:], mvv[:, :, 1], ACT.Sqrt, bias=eps[:]), e)
    e = dve(lambda: V.reciprocal(rstd[:], rstd[:]), e)
    e_xn = []
    for t in range(16):
        e_xn.append(dve(lambda t=t: V.tensor_scalar(xn[:, 128 * t:128 * t + 128], xn[:, 128 * t:128 * t + 128],
                                                  mv[:, 2 * t:2 * t + 1], rstd[:, t:t + 1], ALU.subtract, ALU.mult), e))
    dve(lambda: V.tensor_copy(pm[:], pmcol), e_c)
    e_cb = dve(lambda: V.tensor_copy(cbs[:], tmp[:, 0:B_N]), e_c)
    e_st = sp.dma(lambda: nc.sync.dma_start(xnd.rearrange("(t p) d -> p t d", p=128), xv), d_xn, e_xn[15])
    e_xt = []
    for g in range(4):
        for t in range(4 * g, 4 * g + 4):
            e = pe(lambda t=t, g=g: T.transpose(ps[g][:, 128 * (t % 4):128 * (t % 4) + 128],
                                                xn[:, 128 * t:128 * t + 128], ident[:]), e_xn[t], e_c)
        e_xt.append(act(lambda g=g: A.copy(xnt[:, 512 * g:512 * g + 512], ps[g][:]), e))
        for t in range(4 * g, 4 * g + 4):
            e_sc = pe(lambda t=t: T.matmul(ps[5][:, 8 * t:8 * t + 8], xnt[:, 128 * t:128 * t + 128], et[:],
                                           start=True, stop=True), e_xt[g])

    e = dve(lambda: V.tensor_copy(ball[0:64, :], braw[0:64, :]), e_b)
    e = dve(lambda: V.tensor_copy(btmp[32:64, :], braw[32:64, :]), e)
    e_ball = dve(lambda: V.tensor_tensor(ball[32:64, :], braw[32:64, :], btmp[32:64, :], ALU.subtract), e)

    state = {}
    r3 = lambda ap, a, b: ap.rearrange("p (a b) -> p a b", a=a, b=b)

    def dispatch():
        def step(fn, *needs):
            state["e"] = dve(fn, state.get("e"), *needs)
        scv = r3(sc[:], 16, 8)
        s_oth = scv.unsqueeze(2).to_broadcast([128, 16, 8, 8])
        s_own = scv.unsqueeze(3).to_broadcast([128, 16, 8, 8])
        four = lambda a: a.rearrange("p (t e f) -> p t e f", t=16, e=8)
        step(lambda: V.tensor_copy(sc[:], ps[5][:, 0:128]), e_sc, e_st)
        step(lambda: V.tensor_tensor(four(gt[:]), s_oth, s_own, ALU.is_gt))
        yield
        step(lambda: V.tensor_tensor(four(eq[:]), s_oth, s_own, ALU.is_equal))
        yield
        step(lambda: V.tensor_tensor(r3(eq[:], 16, 64), r3(eq[:], 16, 64),
                                     b_lm.unsqueeze(1).to_broadcast([128, 16, 64]), ALU.mult), e_cb)
        step(lambda: V.tensor_tensor(gt[:], gt[:], eq[:], ALU.add))
        yield
        step(lambda: V.tensor_reduce(s0[:], r3(gt[:], 128, 8), AX.X, ALU.add))
        step(lambda: V.tensor_scalar(msk[:], s0[:], 2.0, None, ALU.is_lt))
        e_m = state["e"]
        mv3 = r3(msk[:], 16, 8)
        pe(lambda: T.matmul(ps[5][:, 0:128], b_tri, msk[:], start=True, stop=False, skip_group_check=True), e_m, sig=False)
        for t in range(16):
            e_p = pe(lambda t=t: T.matmul(
                r3(ps[5][:, 8 * (t + 1):136], 16 - t, 8), b_one,
                mv3[:, t:t + 1, :].to_broadcast([128, 16 - t, 8]), start=False, stop=(t == 15), skip_group_check=True))
        yield
        step(lambda: V.tensor_copy(ne[:], ps[5][:, 128:136]), e_p)
        step(lambda: V.tensor_tensor(r3(cm[:], 8, 16), ne[:].unsqueeze(2).to_broadcast([128, 8, 16]),
                                     k128.unsqueeze(1).to_broadcast([128, 8, 16]), ALU.is_gt))
        step(lambda: V.tensor_reduce(ce[:], r3(cm[:], 8, 16), AX.X, ALU.add))
        step(lambda: V.tensor_tensor(r3(cm[:, 0:64], 8, 8), ce[:].unsqueeze(1).to_broadcast([128, 8, 8]),
                                     r3(lm8, 8, 8), ALU.mult))
        step(lambda: V.tensor_reduce(be[:], r3(cm[:, 0:64], 8, 8), AX.X, ALU.add))
        step(lambda: V.scalar_tensor_tensor(r3(s0[:], 16, 8), be[:].unsqueeze(1).to_broadcast([128, 16, 8]), 128.0,
                                            r3(ps[5][:, 0:128], 16, 8), ALU.mult, ALU.add))
        yield
        step(lambda: V.scalar_tensor_tensor(s1[:], s0[:], 1.0, msk[:], ALU.add, ALU.mult))
        step(lambda: V.tensor_reduce(dst[:, 0:16], r3(s1[:], 16, 8), AX.X, ALU.max))
        step(lambda: V.tensor_scalar(dst[:, 0:16], dst[:, 0:16], -1.0, None, ALU.add))
        step(lambda: V.scalar_tensor_tensor(s1[:], s0[:], -8192.0, msk[:], ALU.add, ALU.mult))
        step(lambda: V.tensor_reduce(dst[:, 16:32], r3(s1[:], 16, 8), AX.X, ALU.min))
        step(lambda: V.tensor_scalar(dst[:, 16:32], dst[:, 16:32], 8192.0, None, ALU.add))
        step(lambda: V.tensor_copy(dsi[:], dst[:]))
        step(lambda: V.tensor_scalar(dhi[:], dsi[:], 7, None, ALU.logical_shift_right))
        step(lambda: V.tensor_scalar(dlo[:], dsi[:], 127, None, ALU.bitwise_and))
        step(lambda: V.tensor_copy(dtf[:], dhi[:]))
        step(lambda: V.tensor_copy(dpf[:], dlo[:]))
        step(lambda: V.memset(ex[:], 0.0))
        for e_ in range(1, 8):
            step(lambda e_=e_: V.scalar_tensor_tensor(ex[:], iot, be[:, e_:e_ + 1], ex[:], ALU.is_ge, ALU.add))
        step(lambda: V.tensor_copy(exi[:], ex[:]))
        yield
        e0 = state["e"]
        used = [None] * 8
        for i in range(32):
            k = i % 8
            t = i % 16
            dve(lambda i=i, k=k: V.tensor_scalar(oh[k][:], b_io, dpf[:, i:i + 1], None, ALU.is_equal), e0, used[k])
            dve(lambda i=i, k=k, t=t: V.tensor_scalar(bt[k][:, 0:NTP], iot, dtf[:, i:i + 1], float(t + 1),
                                                      ALU.is_equal, ALU.mult))
            e = dve(lambda i=i, k=k: V.tensor_scalar(bt[k][:, NTP:2 * NTP], iot, dtf[:, i:i + 1], pcol,
                                                     ALU.is_equal, ALU.mult))
            used[k] = pe(lambda i=i, k=k: T.matmul(ps[5][:, 0:2 * NTP], oh[k][:], bt[k][:], start=(i == 0),
                                                   stop=(i == 31)), e)
            if i % 8 == 7:
                yield
        state["e"] = e
        step(lambda: V.tensor_copy(tbh[:], ps[5][:, 0:2 * NTP]), used[7])
        step(lambda: V.tensor_scalar(tbg[:], tbh[:, 0:NTP], -1.0, 0.0, ALU.add, ALU.max))
        step(lambda: V.scalar_tensor_tensor(tbg[:], tbg[:], 128.0, tbh[:, NTP:2 * NTP], ALU.mult, ALU.add))
        step(lambda: V.tensor_copy(gidx[:], tbg[:]))
        step(lambda: V.tensor_scalar(tbe[:], tbh[:, 0:NTP], 0.0, 4096.0, ALU.is_equal, ALU.mult))
        step(lambda: V.tensor_tensor(tbe[:], tbe[:], tbg[:], ALU.add))
        step(lambda: V.tensor_copy(sidx[:], tbe[:]))
        yield

    disp = dispatch()
    for _ in range(4):
        next(disp)

    ov = out.rearrange("(b c p) d -> b p c d", p=128, c=2)
    xrv = x.rearrange("(b c p) d -> b p c d", p=128, c=2)
    for c in range(2):
        e_vz = dve(lambda c=c: V.memset(vm[c][:], 0.0))
    mm = lambda o_, l, r, s=True, p=True: T.matmul(o_, l, r, start=s, stop=p, skip_group_check=True)
    R = {}

    def proj(b):
        xs = xnt[:, 256 * b:256 * b + 256]
        for n in range(4):
            R["qk", n // 2, b] = pe(lambda n=n: mm(ps[n // 2][:, 256 * (n % 2):256 * (n % 2) + 256],
                                                   wq[:, 128 * n:128 * n + 128], xs),
                                    R.get(("rot", n // 2, b - 1)), e_xt[b // 2], e_c)
        for n, dstb in ((0, qr[b % 2]), (1, kr[b % 2])):
            half = tmp[:, 512 * n:512 * n + 512]
            R["rot", n, b] = dve(lambda n=n, half=half: V.tensor_tensor(
                half, ps[n][:], tab[:, 512 * n:512 * n + 512], ALU.mult), R["qk", n, b], e_cb)
            R["qk_r", n, b] = dve(lambda half=half, dstb=dstb: V.tensor_tensor(
                dstb[:], half[:, 0:256], half[:, 256:512], ALU.add), R["rot", n, b],
                R.get(("cross", b - 1)), R.get(("sc", b - 1 if n == 0 else b - 2)))
        for m in range(4):
            R["qx", b] = act(lambda m=m: A.activation(qx[b % 2][:, 256 * m:256 * m + 256], qr[b % 2][:], ACT.Copy,
                                                      scale=hm(m)), R["qk_r", 0, b], R.get(("sc", b - 2)), e_ball)

    def projv(b):
        for c in range(2):
            R["v", b] = pe(lambda c=c: mm(ps[2][:, 128 * c:128 * c + 128],
                                          xnt[:, 256 * b + 128 * c:256 * b + 128 * c + 128], wv[:, 0:128]),
                           R.get(("smt", b - 1)), R.get(("vcopy", b - 1)))
        for c in range(2):
            dv = vm[c][:].rearrange("p (g q) -> p g q", g=4)
            for m in range(4):
                R["vm", b] = dve(lambda c=c, m=m, dv=dv: V.tensor_copy(
                    dv[:, :, 40 * m:40 * m + 8],
                    ps[2][:, 128 * c:128 * c + 128].rearrange("p (g q) -> p g q", g=4)[:, :, 8 * m:8 * m + 8]),
                    R["v", b], R.get(("av", b - 1)), e_vz)
        R["vcopy", b] = dve(lambda: V.tensor_copy(vs[:], ps[2][:, 0:128]), R["v", b], R.get(("s", b - 1)))

    def ktrans(b):
        e = pe(lambda: T.transpose(ps[2][:, 256:384], kr[b % 2][:, 0:128], ident[:]), R["qk_r", 1, b], R["vcopy", b])
        R["kt", b] = dve(lambda: V.tensor_copy(kt[:], ps[2][:, 256:384]), e, R.get(("s", b - 1)))

    def smat(b):
        R["s", b] = pe(lambda: mm(ps[2][:, 384:512], kt[:], vs[:]), R["kt", b])
        R["smt", b] = dve(lambda: V.tensor_tensor(smt[:], ps[2][:, 384:512], cblk, ALU.mult), R["s", b],
                          R.get(("cross", b - 1)))

    def score(b, i):
        c, g = divmod(i, 4)
        n = 8 * b + i
        bank, rows = 3 + n % 2, slice(32 * g, 32 * g + 32)
        R["sc", b] = pe(lambda: mm(r3(ps[bank][:], 4, 128), kr[b % 2][rows, 128 * c:128 * c + 128],
                                   r3(qx[b % 2][rows, :], 4, 256)[:, :, 128 * c:128 * c + 128]),
                        R["qx", b], R["qk_r", 1, b], R.get(("p", n - 2)))
        R["p", n] = dve(lambda: V.tensor_tensor(r3(pt[n % 3][:], 4, 128), r3(ps[bank][:], 4, 128),
                                                cmask.unsqueeze(1).to_broadcast([128, 4, 128]), ALU.mult),
                        R["sc", b], R.get(("avn", n - 3)), e_ball)

    def cross(b):
        R["cross", b] = pe(lambda: mm(ps[6][:, 128:256], smt[:], qr[b % 2][:, 128:256], True, False), R["smt", b],
                           R.get(("rt", b - 1)))

    def av(b, i):
        c, g = divmod(i, 4)
        n = 8 * b + i
        for m in range(4):
            e = pe(lambda m=m: mm(ps[6][32 * g:32 * g + 32, 128 * c:128 * c + 128],
                                  vm[c][:, 128 * g + 32 * m:128 * g + 32 * m + 32],
                                  pt[n % 3][:, 128 * m:128 * m + 128], c == 0 and m == 0, m == 3),
                   R["p", n], R["vm", b], R.get(("rt", b - 1)))
        R["avn", n] = R["av", b] = e

    def evac(b):
        R["rt", b] = act(lambda: A.copy(rt[:], ps[6][:, 0:256]), R["av", b], R.get(("cen", b - 1)))

    def centre(b):
        R["cen", b] = pe(lambda: mm(ps[7][:, 0:256], ccen, rt[:]), R["rt", b], R.get(("base", b - 1)))
        R["sq", b] = act(lambda: A.activation(sq[:], ps[7][:, 0:256], ACT.Square), R["cen", b], R.get(("var", b - 1)))

    def var(b):
        R["var", b] = pe(lambda: mm(ps[7][:, 256:512], cavg, sq[:]), R["sq", b])
        e = act(lambda: A.activation(rs[:], ps[7][:, 256:512], ACT.Sqrt, bias=eps[:]), R["var", b], R.get(("rn", b - 1)))
        e = dve(lambda: V.reciprocal(rs[:], rs[:]), e)
        e = dve(lambda: V.scalar_tensor_tensor(rn[:], ps[7][:, 0:256], gbt[:, 0:1], rs[:], ALU.mult, ALU.mult), e,
                R.get(("y", b - 1)))
        R["rn", b] = dve(lambda: V.tensor_scalar(rn[:], rn[:], gbt[:, 1:2], None, ALU.add), e)

    def wout(b):
        ld = act.dma(lambda: nc.scalar.dma_start(xr[:].rearrange("p (c d) -> p c d", c=2), xrv[b]), d_xr, R.get(("base", b - 1)))
        for c in range(2):
            R["y", b] = pe(lambda c=c: mm(ps[7][:, 256 + 128 * c:384 + 128 * c], rn[:, 128 * c:128 * c + 128],
                                          wv[:, 128:256]), R["rn", b])
        R["base", b] = dve(lambda: V.tensor_tensor(ob[b % 2][:], ps[7][:, 256:512], xr[:], ALU.add), R["y", b], ld,
                           R.get(("ost", b - 2)))
        R["ost", b] = act.dma(lambda: nc.scalar.dma_start(ov[b], ob[b % 2][:].rearrange("p (c d) -> p c d", c=2)),
                              d_ob[b % 2], R["base", b])

    d_ob = [DmaSem(S(f"d_ob{i}")) for i in range(2)]
    proj(0)
    projv(0)
    for b in range(NB):
        for i in range(8):
            score(b, i)
            if i == 0:
                ktrans(b)
            if i == 1 and b:
                centre(b - 1)
            if i == 2:
                smat(b)
            if i >= 2:
                av(b, i - 2)
            if i == 3 and b:
                var(b - 1)
            if i == 4 and b:
                wout(b - 1)
            if i == 5:
                cross(b)
            if i in (1, 3, 5, 6) and staged[0] < 30:
                stage()
        if b + 1 < NB:
            proj(b + 1)
        av(b, 6)
        av(b, 7)
        evac(b)
        if b + 1 < NB:
            projv(b + 1)
        next(disp, None)
    centre(NB - 1)
    var(NB - 1)
    wout(NB - 1)
    for _ in disp:
        pass
    attn_end = [R["y", NB - 1], R["base", NB - 1], R["rn", NB - 1], R["ost", NB - 1], R["ost", NB - 2], state["e"]]
    while staged[0] < 40:
        stage(after=attn_end)
    e_w3b = act.dma(lambda: nc.scalar.dma_start(
        w3s[:].rearrange("p (e c k) -> p e c k", e=8, c=4)[:, 6:8].rearrange("p e c k -> p (e c) k"),
        w3[6:8].rearrange("e (c p) k -> p (e c) k", p=128)), d_w3, *attn_end)
    weights = [w_done["v"], w_done["p"], e_w3, e_w3b]

    X = {}
    regs = {}
    W = {}

    def gather(t):
        X["g", t] = pool.dma(lambda: nc.gpsimd.indirect_dma_start(
            xg[t % 4][:], None, xnd, bass.IndirectOffsetOnAxis(ap=gidx[:, t:t + 1], axis=0)),
            d_g[t % 4], X.get(("xT", t - 4)), state["e"], e_st, *attn_end, *(weights if t == 2 else []))

    def xtrans(t):
        X["xT", t] = pe(lambda: T.transpose(ps[5][:, 0:128], xg[t % 4][:], ident[:]), X["g", t], X.get(("xl", t - 1)))
        h = act(lambda: A.copy(xh[t % 2][:], ps[5][:, 0:128]), X["xT", t], X.get(("L1", t - 2)))
        X["xl", t] = dve(lambda: V.tensor_tensor(xl[t % 2][:], ps[5][:, 0:128], xh[t % 2][:], ALU.subtract), h)
        X["sel", t] = dve(lambda: V.tensor_scalar(sel[t % 5][0:64, :], ex[0:64, t:t + 1].to_broadcast([64, 128]),
                                                  pm[0:64, :], None, ALU.is_equal), X.get(("L3", t - 5)), *attn_end, *weights)

    def loadreg(t):
        regs[t] = nc.tensor.value_load(exi[0:1, t:t + 1], min_val=0, max_val=7)

    def layer1(t):
        bank = ps[0]
        n = t % 2

        def rhs(w):
            return w[:, bass.ds(regs[t] * 512, 512)]

        def first():
            if t < 2:
                loadreg(t)
            return mm(bank[:], sel[t % 5][0:64, :], ball[0:64, 0:512], True, False)
        pe(first, X["sel", t], X["xl", t], X.get(("g1", t - 1)), *weights, sig=False)
        pe(lambda: mm(bank[:], xh[n][:], rhs(w1l), False, False), sig=False)
        pe(lambda: mm(bank[:], xl[n][:], rhs(w1h), False, False), sig=False)
        X["L1", t] = pe(lambda: mm(bank[:], xh[n][:], rhs(w1h), False, True))
        X["g1", t] = act(lambda: A.activation(g1[:], bank[:], ACT.Gelu), X["L1", t], X.get(("T1", t - 1)))

    def trans1(t):
        for c in range(4):
            X["T1", t] = pe(lambda c=c: T.transpose(ps[1][:, 128 * c:128 * c + 128], g1[:, 128 * c:128 * c + 128],
                                                    ident[:]), X["g1", t], X.get(("h1l", t - 1)))
        h = act(lambda: A.copy(h1h[:], ps[1][:]), X["T1", t], X.get(("L2", t - 1)))
        X["h1l", t] = dve(lambda: V.tensor_tensor(h1l[:], ps[1][:], h1h[:], ALU.subtract), h, X.get(("L2", t - 1)))

    def layer2(t):
        bank = ps[2]
        n = t % 2

        def rhs(w, c):
            return w[:, bass.ds(regs[t] * 2048 + 512 * c, 512)]
        pe(lambda: mm(bank[:], sel[t % 5][0:64, :], ball[0:64, 512:1024], True, False), X.get(("g2", t - 1)), sig=False)
        for c in range(4):
            cc = slice(128 * c, 128 * c + 128)
            pe(lambda c=c, cc=cc: mm(bank[:], h1h[:, cc], rhs(w2l, c), False, False), X["h1l", t], sig=False)
            pe(lambda c=c, cc=cc: mm(bank[:], h1l[:, cc], rhs(w2h, c), False, False), sig=False)
            X["L2", t] = pe(lambda c=c, cc=cc: mm(bank[:], h1h[:, cc], rhs(w2h, c), False, c == 3))
            if c == 1 and t + 2 < NT:
                pe(lambda: loadreg(t + 2), sig=False)
        X["g2", t] = act(lambda: A.activation(g2[:], bank[:], ACT.Gelu), X["L2", t], X.get(("T2", t - 1)))

    def trans2(t):
        for c in range(4):
            X["T2", t] = pe(lambda c=c: T.transpose(ps[3][:, 128 * c:128 * c + 128], g2[:, 128 * c:128 * c + 128],
                                                    ident[:]), X["g2", t], X.get(("h2", t - 1)))
        X["h2", t] = dve(lambda: V.tensor_copy(h2t[t % 2][:], ps[3][:]), X["T2", t], X.get(("L3", t - 2)))

    def layer3(t):
        bank = ps[4][:, 0:128]
        n = t % 2

        def rhs(c):
            return w3s[:, bass.ds(regs[t] * 512 + 128 * c, 128)]
        pe(lambda: mm(bank, sel[t % 5][0:64, :], ball[0:64, 1024:1152], True, False), X.get(("ys", t - 1)), sig=False)
        for c in range(4):
            X["L3", t] = pe(lambda c=c: mm(bank, h2t[n][:, 128 * c:128 * c + 128], rhs(c), False, c == 3), X["h2", t])
        X["ys", t] = dve(lambda: V.tensor_scalar(ys[n][:], bank, 0.5, None, ALU.mult), X["L3", t], X.get(("add", t - 2)))

    def scatter(t):
        X["add", t] = pool.dma(lambda: nc.gpsimd.indirect_dma_start(
            out, bass.IndirectOffsetOnAxis(ap=sidx[:, t:t + 1], axis=0), ys[t % 2][:], None,
            bounds_check=NTOK - 1, oob_is_err=False, compute_op=ALU.add),
            d_s, X["ys", t], X.get(("add", t - 1)), *attn_end)

    gather(0)
    gather(1)
    xtrans(0)
    layer1(0)
    gather(2)
    gather(3)
    xtrans(1)
    trans1(0)
    layer1(1)
    xtrans(2)
    for t in range(NT):
        if t + 4 < NT:
            gather(t + 4)
        layer2(t)
        if t + 1 < NT:
            trans1(t + 1)
        if t + 3 < NT:
            xtrans(t + 3)
        if t + 2 < NT:
            layer1(t + 2)
        trans2(t)
        if t:
            layer3(t - 1)
            scatter(t - 1)
    layer3(NT - 1)
    scatter(NT - 1)
    pool.ops.append((lambda: None, [X["add", NT - 1]], False))

    with nc.Block() as block:
        @block.sync
        def _(eng):
            sp.emit(eng)

        @block.scalar
        def _(eng):
            act.emit(eng)

        @block.vector
        def _(eng):
            dve.emit(eng)

        @block.gpsimd
        def _(eng):
            pool.emit(eng)

        @block.tensor
        def _(eng):
            pe.emit(eng)


def kernel(**inputs):
    import concourse.bacc as bacc
    from concourse.bass_utils import run_bass_kernel_spmd

    a = {k: np.asarray(v) for k, v in inputs.items()}
    swap = np.arange(128) ^ 1
    wqT = a["L0_attn_WQ"].reshape(128, 128).T
    wkT = a["L0_attn_WK"].reshape(128, 128).T
    wvT = a["L0_attn_WV"].reshape(128, 128).T
    cf, cb = constants()
    arrays = {
        "x": a["L0_attn_x"].reshape(NTOK, D),
        "wqkv": np.concatenate([wqT, wqT[:, swap], wkT, wkT[:, swap]], axis=1),
        "wvo": np.concatenate([wvT, a["L0_attn_WO"]], axis=1),
        "gb": np.stack([a["L0_attn_gamma"], a["L0_attn_beta"]], axis=1),
        "etokT": a["L0_ffn_expert_tokens"].T,
        "w1": a["L0_ffn_W1"], "w2": a["L0_ffn_W2"], "w3": a["L0_ffn_W3"],
        "bias": np.concatenate([a["L0_ffn_b1"], a["L0_ffn_b2"], a["L0_ffn_b3"]], axis=1),
        "cf": cf, "cb": cb,
    }
    arrays = {k: np.ascontiguousarray(v) for k, v in arrays.items()}
    nc = bacc.Bacc("TRN2", target_bir_lowering=False, num_devices=1)
    aps = {k: nc.dram_tensor(f"in_{k}", v.shape, mybir.dt.from_np(v.dtype), kind="ExternalInput").ap()
           for k, v in arrays.items()}
    out = nc.dram_tensor("out_0", (NTOK, D), F32, kind="ExternalOutput").ap()
    moe_retention_kernel(nc, *aps.values(), out)
    r = run_bass_kernel_spmd(nc, [{f"in_{k}": v for k, v in arrays.items()}], core_ids=[0])
    return r.results[0]["out_0"].reshape(8, 256, 128)
```

```python
import numpy as np
import concourse.bass as bass
from concourse import mybir

F32 = mybir.dt.float32
F32R = mybir.dt.float32r
BF16 = mybir.dt.bfloat16
I32 = mybir.dt.int32
U32 = mybir.dt.uint32
ALU = mybir.AluOpType
ACT = mybir.ActivationFunctionType
AX = mybir.AxisListType

NTOK, D, HID, NEXP = 2048, 128, 512, 8
NTT = NTOK // 128
NB, SEQ, NHEAD = 8, 256, 16
NT = 39
NTP = 40
LATE = 3

C_ID, C_MASK, C_BLK, C_CEN, C_AVG = 0, 128, 256, 384, 512
C_TAB = 640
C_HM = 1664
C_P, C_PM = 1668, 1669
C_IT = 1670
C_K = 1710
C_L = 1726
C_REP = 1790
C_N = 2302
B_IO, B_TRI, B_ONE, B_LM = 0, 128, 256, 384
B_N = 448


def constants():
    c = np.zeros((128, C_N), np.float32)
    p = np.arange(128)
    c[:, C_ID:C_ID + 128] = np.eye(128)
    c[:, C_MASK:C_MASK + 128] = p[None, :] >= p[:, None]
    same = (p[:, None] // 8) == (p[None, :] // 8)
    c[:, C_BLK:C_BLK + 128] = same
    c[:, C_CEN:C_CEN + 128] = np.eye(128) - same / 8.0
    c[:, C_AVG:C_AVG + 128] = same / 8.0
    ex = np.arange(0, 8, 2, dtype=np.float32) / np.float32(8)
    angle = np.power(np.float32(10.0), np.float32(-4.0) * ex).astype(np.float32)
    pos = np.arange(SEQ, dtype=np.float32)
    ang = (pos[None, :] * angle[(p % 8) // 2][:, None]).astype(np.float32).astype(np.float64)
    sgn = np.where(p % 2 == 0, -1.0, 1.0)[:, None]
    g = (1.0 - 2.0 ** (-5.0 - (p // 8)))[:, None]
    up, down = g ** pos[None, :], g ** -pos[None, :].astype(np.float64)
    for n, t in enumerate((np.cos(ang) * up, np.sin(ang) * sgn * up, np.cos(ang) * down, np.sin(ang) * sgn * down)):
        c[:, C_TAB + 256 * n:C_TAB + 256 * (n + 1)] = t
    for m in range(4):
        c[:, C_HM + m] = ((p // 8) % 4) == m
    c[:, C_P] = p
    c[:, C_PM] = p % 32
    c[:, C_IT:C_IT + NTP] = np.arange(NTP)
    c[:, C_K:C_K + 16] = 128 * np.arange(16)
    e = np.arange(8)
    c[:, C_L:C_L + 64] = (e[None, :] < e[:, None]).reshape(1, 64)
    m, part, u = p // 32, (p // 8) % 4, p % 8
    for n, use in enumerate((part < 2, part >= 2, part % 2 == 0, part % 2 == 1)):
        c[:, C_REP + 128 * n:C_REP + 128 * (n + 1)] = ((p[:, None] % 32) == (8 * m + u)[None, :]) & use[None, :]
    b = np.zeros((128, B_N), np.float32)
    b[:, B_IO:B_IO + 128] = p[None, :]
    b[:, B_TRI:B_TRI + 128] = p[:, None] < p[None, :]
    b[:, B_ONE:B_ONE + 128] = 1
    b[:, B_LM:B_LM + 64] = (e[None, :] < e[:, None]).reshape(1, 64)
    return c, b


class Queue:

    def __init__(self, sem):
        self.sem, self.n, self.ops = sem, 0, []

    def __call__(self, fn, *needs, sig=True):
        self.ops.append((fn, [x for x in needs if x is not None], sig))
        if sig:
            self.n += 1
            return (self.sem, self.n)

    def dma(self, fn, done, *needs):
        self.ops.append((fn, [x for x in needs if x is not None], done.sem))
        done.n += 16
        return (done.sem, done.n)

    def emit(self, eng):
        seen = {}
        for fn, needs, sig in self.ops:
            for sem, value in needs:
                if seen.get(sem.name, 0) < value:
                    eng.wait_ge(sem, value)
                    seen[sem.name] = value
            ins = fn()
            if sig is True:
                ins.then_inc(self.sem, 1)
            elif sig is not False:
                ins.then_inc(sig, 16)


class DmaSem:
    def __init__(self, sem):
        self.sem, self.n = sem, 0


def moe_retention_kernel(nc, x, wqkv, wvo, gb, etokT, w1, w2, w3, bias, cf, cb, out):
    def at(name, cols, dt, off, parts=128):
        return nc.alloc_sbuf_tensor_at(name, [parts, cols], dt, offset=off)

    R0 = 16512
    W2H, W2L = R0, R0 + 65536
    W1H, W1L, W3O = R0 + 131072, R0 + 147456, R0 + 163840
    BO = R0 + 180224
    F0 = BO + 4608
    w2h = at("w2h", 8 * 2048, F32R, W2H)
    w2l = at("w2l", 8 * 2048, F32R, W2L)
    w1h = at("w1h", 8 * 512, F32R, W1H)
    w1l = at("w1l", 8 * 512, F32R, W1L)
    w3s = at("w3s", 8 * 512, F32, W3O)
    ball = at("ball", 1152, F32R, BO)
    o = F0
    ident = at("ident", 128, F32, o); o += 512
    gidx = at("gidx", NTP, U32, o); o += 160
    sidx = at("sidx", NTP, U32, o); o += 160
    ex = at("ex", NTP, F32, o); o += 160
    exi = at("exi", NTP, I32, o); o += 160
    pm = at("pm", 1, F32, o); o += 32
    stg = [at(f"stg{i}", 512, F32, o + 2048 * i) for i in range(4)]; o += 8192
    G0 = o
    xg = [at(f"xg{i}", 128, F32, (o if i < 2 else G0 - 4096 - 1024) + 512 * i) for i in range(4)]; o += 1024
    xh = [at(f"xh{i}", 128, F32R, o + 1024 * i) for i in range(2)]
    xl = [at(f"xl{i}", 128, F32R, o + 512 + 1024 * i) for i in range(2)]; o += 2048
    g1 = at("g1", 512, F32, o); o += 2048
    h1h = at("h1h", 512, F32R, o); o += 2048
    h1l = at("h1l", 512, F32R, o); o += 2048
    g2 = at("g2", 512, F32, o); o += 2048
    h2t = [at(f"h2t{i}", 512, F32, o + 2048 * i) for i in range(2)]; o += 4096
    ys = [at(f"ys{i}", 128, F32, o + 512 * i) for i in range(2)]; o += 1024
    sel = [at(f"sel{i}", 128, F32R, G0 - 8192 + 512 * i) for i in range(5)]
    assert o <= 229368
    o = G0
    cs = at("cs", 512, F32, o); o += 2048
    small = at("small", C_REP - C_HM, F32, o); o += 512
    cbs = at("cbs", B_N, BF16, o); o += 896
    wq = at("wq", 512, F32, o); o += 2048
    wv = at("wv", 256, F32, o); o += 1024
    gbt = at("gbt", 2, F32, o); o += 32
    et = at("et", 8, F32, o); o += 32
    xr = at("xr", 256, F32, o); o += 1024
    vs = at("vs", 128, F32, o); o += 512
    rt = at("rt", 256, F32, o); o += 1024
    sq = at("sq", 256, F32, o); o += 1024
    rs = at("rs", 256, F32, o); o += 1024
    rn = at("rn", 256, F32, o); o += 1024
    ob = [at(f"ob{i}", 256, F32, o) for i in range(1)] * 2; o += 1024
    qr = [at("qr0", 256, F32, o), at("qr1", 256, F32, o + 1024)]; o += 2048
    kr = [at("kr0", 256, F32, o), at("kr1", 256, F32, o + 1024)]; o += 2048
    st = at("st", 96, F32, o); o += 384
    mv = at("mv", 32, F32, o); o += 128
    rstd = at("rstd", 16, F32, o); o += 64
    eps = at("eps", 1, F32, o); o += 32
    assert o <= 229368, o
    A0 = W2H + 40960
    B0 = W2L + 40960
    C0, D0, E0 = W1H + 10240, W1L + 10240, W3O + 10240
    o = A0
    oh = [at(f"oh{i}", 128, BF16, o + 256 * i) for i in range(8)]; o += 2048
    bt = at("bt", 16 * NTP, BF16, o); o += 1280
    s1 = at("s1", 128, F32, A0)
    cm = at("cm", 128, F32, A0 + 512)
    sc = at("sc", 128, F32, A0 + 1024)
    s0 = at("s0", 128, F32, A0 + 1536)
    msk = at("msk", 128, BF16, A0 + 2048)
    ne = at("ne", 8, F32, A0 + 2304)
    ce = at("ce", 8, F32, A0 + 2336)
    be = at("be", 8, F32, A0 + 2368)
    dst = at("dst", 32, F32, A0 + 2400)
    dsi = at("dsi", 32, I32, A0 + 2528)
    dhi = at("dhi", 32, I32, A0 + 2656)
    dlo = at("dlo", 32, I32, A0 + 2784)
    dtf = at("dtf", 32, F32, o); o += 128
    dpf = at("dpf", 32, F32, o); o += 128
    tbh = at("tbh", 2 * NTP, F32, o); o += 320
    tbg = at("tbg", NTP, F32, o); o += 160
    tbe = at("tbe", NTP, F32, o - 480 - 256)
    assert o <= A0 + 4096
    xnt = at("xnt", 2048, F32, A0 + 4096)
    pt = [at(f"pt{i}", 512, F32, A0 + 12288 + 2048 * i) for i in range(6)]
    braw = at("braw", 1152, F32, A0 + 12288)
    btmp = at("btmp", 1152, F32R, A0 + 12288 + 4608)
    qx = at("qx", 4096, F32R, B0)
    xn = at("xn", 2048, F32, B0)
    kst = [at(f"kst{i}", 1024, F32R, B0 + 16384 + 4096 * i) for i in range(2)]
    gt = at("gt", 1024, BF16, B0 + 20480)
    eq = at("eq", 1024, BF16, B0 + 22528)
    vm = [at(f"vm{i}", 640, F32, C0 + 2560 * i) for i in range(2)]
    kt = at("kt", 128, F32, C0 + 5120)
    smt = at("smt", 128, F32, C0 + 5632)
    tab = at("tab", 1024, F32, D0)
    qh = at("qh", 256, F32R, D0 + 4096)
    ql = at("ql", 256, F32R, D0 + 5120)
    tmp = at("tmp", 512, F32, E0)
    repf = at("repf", 512, F32, A0 + 12288 + 10240)
    repm = at("repm", 512, F32R, E0 + 2048)
    kh = at("kh", 256, F32R, E0 + 4096)
    kl = at("kl", 256, F32R, E0 + 5120)
    ps = [nc.alloc_psum_tensor(f"ps{i}", [128, 512], F32) for i in range(8)]
    xnd = nc.dram_tensor("xnd", (NTOK, D), F32, kind="Internal").ap()

    cmask, cblk, ccen, cavg = (cs[:, 128 * i:128 * i + 128] for i in range(4))
    hm = lambda m: small[:, m:m + 1]
    pcol = small[:, C_P - C_HM:C_P - C_HM + 1]
    pmcol = small[:, C_PM - C_HM:C_PM - C_HM + 1]
    iot = small[:, C_IT - C_HM:C_IT - C_HM + NTP]
    k128 = small[:, C_K - C_HM:C_K - C_HM + 16]
    lm8 = small[:, C_L - C_HM:C_L - C_HM + 64]
    b_io, b_tri, b_one = (cbs[:, 128 * i:128 * i + 128] for i in range(3))
    b_lm = cbs[:, B_LM:B_LM + 64]

    S = lambda name: nc.alloc_semaphore(name)
    pe, act, dve, pool, sp = (Queue(S(f"q_{n}")) for n in ("pe", "act", "dve", "pool", "sp"))
    d_const, d_x, d_xn = DmaSem(S("d_const")), DmaSem(S("d_x")), DmaSem(S("d_xn"))
    d_bias, d_w3, d_base = DmaSem(S("d_bias")), DmaSem(S("d_w3")), DmaSem(S("d_base"))
    d_xr = DmaSem(S("d_xr"))
    d_stg = [DmaSem(S(f"d_stg{i}")) for i in range(4)]
    d_g = [DmaSem(S(f"d_g{i}")) for i in range(4)]
    d_s = DmaSem(S("d_s"))
    V, A, G, T = nc.vector, nc.scalar, nc.gpsimd, nc.tensor

    xt = x.rearrange("(t p) d -> p t d", p=128)
    xv = xn[:].rearrange("p (t d) -> p t d", d=128)
    d_x4 = [DmaSem(S(f"d_x{i}")) for i in range(4)]
    e_x = []
    for i in range(4):
        e_x.append(sp.dma(lambda i=i: nc.sync.dma_start(xv[:, 4 * i:4 * i + 4, :], xt[:, 4 * i:4 * i + 4, :]), d_x4[i]))
    for dst_, src_ in ((ident[:], cf[:, 0:128]), (cs[:], cf[:, 128:640]), (small[:], cf[:, C_HM:C_REP]),
                       (tmp[:, 0:B_N], cb), (et[:], etokT), (wq[:], wqkv), (wv[:], wvo), (gbt[:], gb),
                       (tab[:], cf[:, C_TAB:C_TAB + 1024]), (repf[:], cf[:, C_REP:C_N])):
        e_c = act.dma(lambda a=dst_, b=src_: nc.scalar.dma_start(a, b), d_const)
    e_z = dve(lambda: V.memset(braw[0:64, :], 0.0))
    for c in range(2):
        e_vz = pool(lambda c=c: G.memset(vm[c][:], 0.0))
    act.dma(lambda: nc.scalar.dma_start(braw[0:8, :], bias), d_bias, e_z)
    e_b = act.dma(lambda: nc.scalar.dma_start(braw[32:40, :], bias), d_bias, e_z)
    e_w3 = act.dma(lambda: nc.scalar.dma_start(
        w3s[:].rearrange("p (e c k) -> p e c k", e=8, c=4)[:, 0:8 - LATE].rearrange("p e c k -> p (e c) k"),
        w3[0:8 - LATE].rearrange("e (c p) k -> p (e c) k", p=128)), d_w3)

    w2src = w2.rearrange("e (c p) k -> e c p k", p=128)
    pieces = []
    for e in range(8):
        for c in range(4):
            pieces.append((w2src[e, c], w2h[:, e * 2048 + c * 512:][:, 0:512], w2l[:, e * 2048 + c * 512:][:, 0:512]))
        pieces.append((w1[e], w1h[:, e * 512:(e + 1) * 512], w1l[:, e * 512:(e + 1) * 512]))
    last_lo = [None] * 4
    staged = [0]
    w_done = {}

    EARLY = 5 * (8 - LATE)

    def stage(after=()):
        i = staged[0]
        staged[0] += 1
        src, hi, lo = pieces[i]
        b = i % 4
        ld = sp.dma(lambda: nc.sync.dma_start(stg[b][:], src), d_stg[b], last_lo[b])
        h = act(lambda: A.copy(hi, stg[b][:]), ld, *after)
        w_done["h"] = h
        if i >= EARLY and i % 3:
            last_lo[b] = dve(lambda: V.tensor_tensor(lo, stg[b][:], hi, ALU.subtract), h)
            w_done["v"] = last_lo[b]
        else:
            last_lo[b] = pool(lambda: G.tensor_tensor(lo, stg[b][:], hi, ALU.subtract), h)
            w_done["p"] = last_lo[b]

    e_eps = dve(lambda: V.memset(eps[:], 1e-5))
    for t in range(16):
        e = dve(lambda t=t: V.bn_stats(st[:, 6 * t:6 * t + 6], xn[:, 128 * t:128 * t + 128]), e_x[t // 4])
    for t in range(16):
        e = dve(lambda t=t: V.bn_aggr(mv[:, 2 * t:2 * t + 2], st[:, 6 * t:6 * t + 6]), e)
    mvv = mv[:].rearrange("p (t k) -> p t k", k=2)
    e = act(lambda: A.activation(rstd[:], mvv[:, :, 1], ACT.Sqrt, bias=eps[:]), e)
    e = dve(lambda: V.reciprocal(rstd[:], rstd[:]), e)
    e_xn = []
    for t in range(16):
        e_xn.append(dve(lambda t=t: V.tensor_scalar(xn[:, 128 * t:128 * t + 128], xn[:, 128 * t:128 * t + 128],
                                                  mv[:, 2 * t:2 * t + 1], rstd[:, t:t + 1], ALU.subtract, ALU.mult), e))
    dve(lambda: V.tensor_copy(pm[:], pmcol), e_c)
    e_cb = dve(lambda: V.tensor_copy(cbs[:], tmp[:, 0:B_N]), e_c)
    e_rep = dve(lambda: V.tensor_copy(repm[:], repf[:]), e_c)
    e_st = sp.dma(lambda: nc.sync.dma_start(xnd.rearrange("(t p) d -> p t d", p=128), xv), d_xn, e_xn[15])
    e_xt = []
    for g in range(4):
        for t in range(4 * g, 4 * g + 4):
            e = e_tr = pe(lambda t=t, g=g: T.transpose(ps[g][:, 128 * (t % 4):128 * (t % 4) + 128],
                                                xn[:, 128 * t:128 * t + 128], ident[:]), e_xn[t], e_c)
        e_xt.append(act(lambda g=g: A.copy(xnt[:, 512 * g:512 * g + 512], ps[g][:]), e))
        for t in range(4 * g, 4 * g + 4):
            e_sc = pe(lambda t=t: T.matmul(ps[5][:, 8 * t:8 * t + 8], xnt[:, 128 * t:128 * t + 128], et[:],
                                           start=True, stop=True), e_xt[g])

    e_qz = pool(lambda: G.memset(qx[:].bitcast(F32), 0.0), e_st, e_tr)

    e = dve(lambda: V.tensor_copy(ball[0:64, :], braw[0:64, :]), e_b)
    e = dve(lambda: V.tensor_copy(btmp[32:64, :], braw[32:64, :]), e)
    e_ball = dve(lambda: V.tensor_tensor(ball[32:64, :], braw[32:64, :], btmp[32:64, :], ALU.subtract), e)

    state = {}
    r3 = lambda ap, a, b: ap.rearrange("p (a b) -> p a b", a=a, b=b)

    def dispatch():
        def step(fn, *needs):
            state["e"] = dve(fn, state.get("e"), *needs)
        scv = r3(sc[:], 16, 8)
        s_oth = scv.unsqueeze(2).to_broadcast([128, 16, 8, 8])
        s_own = scv.unsqueeze(3).to_broadcast([128, 16, 8, 8])
        four = lambda a: a.rearrange("p (t e f) -> p t e f", t=16, e=8)
        step(lambda: V.tensor_copy(sc[:], ps[5][:, 0:128]), e_sc, e_st)
        step(lambda: V.tensor_tensor(four(gt[:]), s_oth, s_own, ALU.is_gt))
        yield
        step(lambda: V.tensor_tensor(four(eq[:]), s_oth, s_own, ALU.is_equal))
        yield
        step(lambda: V.tensor_tensor(r3(eq[:], 16, 64), r3(eq[:], 16, 64),
                                     b_lm.unsqueeze(1).to_broadcast([128, 16, 64]), ALU.mult), e_cb)
        step(lambda: V.tensor_tensor(gt[:], gt[:], eq[:], ALU.add))
        yield
        step(lambda: V.tensor_reduce(s0[:], r3(gt[:], 128, 8), AX.X, ALU.add))
        R["gt"] = state["e"]
        step(lambda: V.tensor_scalar(msk[:], s0[:], 2.0, None, ALU.is_lt))
        e_m = state["e"]
        mv3 = r3(msk[:], 16, 8)
        pe(lambda: T.matmul(ps[5][:, 0:128], b_tri, msk[:], start=True, stop=False, skip_group_check=True), e_m, sig=False)
        for t in range(16):
            e_p = pe(lambda t=t: T.matmul(
                r3(ps[5][:, 8 * (t + 1):136], 16 - t, 8), b_one,
                mv3[:, t:t + 1, :].to_broadcast([128, 16 - t, 8]), start=False, stop=(t == 15), skip_group_check=True))
        yield
        step(lambda: V.tensor_copy(ne[:], ps[5][:, 128:136]), e_p)
        step(lambda: V.tensor_tensor(r3(cm[:], 8, 16), ne[:].unsqueeze(2).to_broadcast([128, 8, 16]),
                                     k128.unsqueeze(1).to_broadcast([128, 8, 16]), ALU.is_gt))
        step(lambda: V.tensor_reduce(ce[:], r3(cm[:], 8, 16), AX.X, ALU.add))
        step(lambda: V.tensor_tensor(r3(cm[:, 0:64], 8, 8), ce[:].unsqueeze(1).to_broadcast([128, 8, 8]),
                                     r3(lm8, 8, 8), ALU.mult))
        step(lambda: V.tensor_reduce(be[:], r3(cm[:, 0:64], 8, 8), AX.X, ALU.add))
        step(lambda: V.scalar_tensor_tensor(r3(s0[:], 16, 8), be[:].unsqueeze(1).to_broadcast([128, 16, 8]), 128.0,
                                            r3(ps[5][:, 0:128], 16, 8), ALU.mult, ALU.add))
        yield
        step(lambda: V.scalar_tensor_tensor(s1[:], s0[:], 1.0, msk[:], ALU.add, ALU.mult))
        step(lambda: V.tensor_reduce(dst[:, 0:16], r3(s1[:], 16, 8), AX.X, ALU.max))
        step(lambda: V.tensor_scalar(dst[:, 0:16], dst[:, 0:16], -1.0, None, ALU.add))
        step(lambda: V.scalar_tensor_tensor(s1[:], s0[:], -8192.0, msk[:], ALU.add, ALU.mult))
        step(lambda: V.tensor_reduce(dst[:, 16:32], r3(s1[:], 16, 8), AX.X, ALU.min))
        step(lambda: V.tensor_scalar(dst[:, 16:32], dst[:, 16:32], 8192.0, None, ALU.add))
        step(lambda: V.tensor_copy(dsi[:], dst[:]))
        step(lambda: V.tensor_scalar(dhi[:], dsi[:], 7, None, ALU.logical_shift_right))
        step(lambda: V.tensor_scalar(dlo[:], dsi[:], 127, None, ALU.bitwise_and))
        step(lambda: V.tensor_copy(dtf[:], dhi[:]))
        step(lambda: V.tensor_copy(dpf[:], dlo[:]))
        step(lambda: V.memset(ex[:], 0.0))
        for e_ in range(1, 8):
            step(lambda e_=e_: V.scalar_tensor_tensor(ex[:], iot, be[:, e_:e_ + 1], ex[:], ALU.is_ge, ALU.add))
        step(lambda: V.tensor_copy(exi[:], ex[:]))
        yield
        e0, used = state["e"], None
        bt3 = bt[:].rearrange("p (i k c) -> p i k c", i=8, k=2)
        for j in range(4):
            i8 = slice(8 * j, 8 * j + 8)
            t1 = iot[:, 8 * (j % 2) + 1:8 * (j % 2) + 9]
            e = dve(lambda i8=i8: V.tensor_tensor(bt3[:, :, 1, :], iot.unsqueeze(1).to_broadcast([128, 8, NTP]),
                                                  dtf[:, i8].unsqueeze(2).to_broadcast([128, 8, NTP]), ALU.is_equal),
                    e0, used)
            dve(lambda t1=t1: V.tensor_tensor(bt3[:, :, 0, :], bt3[:, :, 1, :],
                                              t1.unsqueeze(2).to_broadcast([128, 8, NTP]), ALU.mult), e)
            dve(lambda: V.tensor_scalar(bt3[:, :, 1, :], bt3[:, :, 1, :], pcol, None, ALU.mult), e)
            for i in range(8 * j, 8 * j + 8):
                e = dve(lambda i=i: V.tensor_scalar(oh[i % 8][:], b_io, dpf[:, i:i + 1], None, ALU.is_equal), used)
            yield
            for i in range(8 * j, 8 * j + 8):
                used = pe(lambda i=i: T.matmul(r3(ps[5][:, 0:2 * NTP], 2, NTP), oh[i % 8][:], bt3[:, i % 8],
                                               start=(i == 0), stop=(i == 31)), e)
        state["e"] = e
        step(lambda: V.tensor_copy(tbh[:], ps[5][:, 0:2 * NTP]), used)
        step(lambda: V.tensor_scalar(tbg[:], tbh[:, 0:NTP], -1.0, 0.0, ALU.add, ALU.max))
        step(lambda: V.scalar_tensor_tensor(tbg[:], tbg[:], 128.0, tbh[:, NTP:2 * NTP], ALU.mult, ALU.add))
        step(lambda: V.tensor_copy(gidx[:], tbg[:]))
        step(lambda: V.tensor_scalar(tbe[:], tbh[:, 0:NTP], 0.0, 4096.0, ALU.is_equal, ALU.mult))
        step(lambda: V.tensor_tensor(tbe[:], tbe[:], tbg[:], ALU.add))
        step(lambda: V.tensor_copy(sidx[:], tbe[:]))
        yield

    disp = dispatch()

    ov = out.rearrange("(b c p) d -> b p c d", p=128, c=2)
    xrv = x.rearrange("(b c p) d -> b p c d", p=128, c=2)
    mm = lambda o_, l, r, s=True, p=True: T.matmul(o_, l, r, start=s, stop=p, skip_group_check=True)
    R = {}
    d_ob = DmaSem(S("d_ob"))
    tabv = {0: tab[:, 0:512], 1: tab[:, 512:1024]}

    def proj(b, n):
        xs = xnt[:, 256 * b:256 * b + 256]
        for k in range(2):
            e = pe(lambda k=k: mm(ps[n][:, 256 * k:256 * k + 256], wq[:, 256 * n + 128 * k:256 * n + 128 * k + 128], xs),
                   R.get(("qx", n, b - 1)), e_xt[b // 2], e_c)
        dstb = (qr, kr)[n][b % 2]
        hi, lo = ((qh, ql), (kh, kl))[n]
        e = dve(lambda: V.tensor_tensor(tmp[:], ps[n][:], tabv[n], ALU.mult), e, e_cb, R.get("tmp"))
        R["tmp"] = R["rot", n, b] = dve(lambda: V.tensor_tensor(dstb[:], tmp[:, 0:256], tmp[:, 256:512], ALU.add), e,
                                        R.get(("cross", b - 2)), R.get(("kt", b - 2)))
        e = act(lambda: A.copy(hi[:], dstb[:]), R["tmp"], R.get(("rep", n, b - 1)))
        R["lo", n, b] = pool(lambda: G.tensor_tensor(lo[:], dstb[:], hi[:], ALU.subtract), e, R.get(("rep", n, b - 1)))

    def stack(b, n):
        hi, lo = ((qh, ql), (kh, kl))[n]
        for g in range(4):
            rows, cols = slice(32 * g, 32 * g + 32), slice(256 * (g // 2), 256 * (g // 2) + 256)
            for k, (src, s_) in enumerate(((hi, True), (lo, False))):
                w = repm[rows, 256 * n + 128 * k:256 * n + 128 * k + 128]
                R["rep", n, b] = pe(lambda g=g, src=src, s_=s_, w=w, rows=rows, cols=cols: mm(
                    ps[g % 2][:, cols], w, src[rows, :], s_, not s_), R["lo", n, b],
                    R["repg", n, g - 2, b] if g > 1 else None, R["rot", 0, b], R["rot", 1, b],
                    R.get(("stk", 1, b)) if n == 0 else None, R.get(("stkv", b)) if n == 0 else None, e_rep)
            R["repg", n, g, b] = R["rep", n, b]

    def unstack_k(b):
        for i in range(2):
            R["stk", 1, b] = act(lambda i=i: A.copy(
                kst[b % 2][:].rearrange("p (j i c) -> p j i c", j=2, i=2)[:, :, i, :], r3(ps[i][:], 2, 256)),
                                 R["repg", 1, 2 + i, b], R.get(("sc", b - 2)), R.get("gt"))

    def unstack_q(b):
        qv = qx[:].rearrange("p (j i m c) -> p j i m c", j=2, i=2, m=4)
        for i, eng, copy in ((0, act, A.copy), (1, dve, V.tensor_copy)):
            for m in range(4):
                rows = slice(32 * m, 32 * m + 32)
                e = eng(lambda i=i, m=m, rows=rows, copy=copy: copy(
                    qv[rows, :, i, m, :], r3(ps[i][rows, :], 2, 256)),
                    R["repg", 0, 2 + i, b], R.get(("sc", b - 1)), e_qz)
            R["qx", i, b] = e
        R["stk", 0, b] = R["qx", 0, b]
        R["stkd", b] = R["qx", 1, b]

    def projv(b):
        for c in range(2):
            e = pe(lambda c=c: mm(ps[2][:, 128 * c:128 * c + 128],
                                  xnt[:, 256 * b + 128 * c:256 * b + 128 * c + 128], wv[:, 0:128]),
                   R.get(("smt", b - 1)))
        for c in range(2):
            R["vm", b] = act(lambda c=c: A.copy(
                vm[c][:].rearrange("p (g m u) -> p g m u", g=4, m=4)[:, :, :, 0:8],
                ps[2][:, 128 * c:128 * c + 128].rearrange("p (g m u) -> p g m u", g=4, m=4)),
                e, R.get(("av", b - 1)), e_vz)
        R["vs", b] = act(lambda: A.copy(vs[:], ps[2][:, 0:128]), e, R.get(("s", b - 1)))

    def ktrans(b):
        e = pe(lambda: T.transpose(ps[2][:, 256:384], kr[b % 2][:, 0:128], ident[:]), R["rot", 1, b], R["vs", b])
        R["kt", b] = act(lambda: A.copy(kt[:], ps[2][:, 256:384]), e, R.get(("s", b - 1)))

    def smat(b):
        R["s", b] = pe(lambda: mm(ps[2][:, 384:512], kt[:], vs[:]), R["kt", b])
        R["smt", b] = dve(lambda: V.tensor_tensor(smt[:], ps[2][:, 384:512], cblk, ALU.mult), R["s", b],
                          R.get(("cross", b - 1)))

    def score(b, i):
        c, g = divmod(i, 4)
        n = 8 * b + i
        bank, p = 3 + n % 2, pt[n % 6]
        qv = qx[:].rearrange("p (g m c i) -> p g m c i", g=4, m=4, c=2)
        R["sc", b] = pe(lambda: mm(r3(ps[bank][:], 4, 128), kst[b % 2][:, 256 * g + 128 * c:256 * g + 128 * c + 128],
                                   qv[:, g, :, c, :]),
                        R["qx", g % 2, b], R["stk", 1, b], R.get(("evac", n - 2)))
        if g == 3 or i == 2:
            e = R["evac", n] = act(lambda: A.copy(p[:], ps[bank][:]), R["sc", b], R.get(("avn", n - 6)), e_ball)
            R["p", n] = pool(lambda: G.affine_select(out=r3(p[:], 4, 128), in_=r3(p[:], 4, 128),
                                                     compare_op=ALU.is_ge, fill=0.0, base=0,
                                                     pattern=[[0, 4], [1, 128]], channel_multiplier=-1), e)
        else:
            R["p", n] = R["evac", n] = dve(lambda: V.tensor_tensor(
                r3(p[:], 4, 128), r3(ps[bank][:], 4, 128), cmask.unsqueeze(1).to_broadcast([128, 4, 128]), ALU.mult),
                R["sc", b], R.get(("avn", n - 6)), e_ball, e_rep)

    def cross(b):
        R["cross", b] = pe(lambda: mm(ps[6][:, 128:256], smt[:], qr[b % 2][:, 128:256], True, False), R["smt", b],
                           R.get(("rt", b - 1)))

    def av(b, c):
        for m in range(4):
            for g in range(4):
                n = 8 * b + 4 * c + g
                e = pe(lambda m=m, g=g, n=n: mm(ps[6][32 * g:32 * g + 32, 128 * c:128 * c + 128],
                                                vm[c][:, 160 * g + 32 * m:160 * g + 32 * m + 32],
                                                pt[n % 6][:, 128 * m:128 * m + 128], c == 0 and m == 0, m == 3),
                       R["p", n], R["vm", b], R.get(("rt", b - 1)))
                R["avn", n] = R["av", b] = e

    def evac(b):
        R["rt", b] = act(lambda: A.copy(rt[:], ps[6][:, 0:256]), R["av", b], R.get(("cen", b - 1)))

    def centre(b):
        R["cen", b] = pe(lambda: mm(ps[7][:, 0:256], ccen, rt[:]), R["rt", b], R.get(("base", b - 1)))
        R["sq", b] = act(lambda: A.activation(sq[:], ps[7][:, 0:256], ACT.Square), R["cen", b], R.get(("var", b - 1)))

    def var(b):
        R["var", b] = pe(lambda: mm(ps[7][:, 256:512], cavg, sq[:]), R["sq", b])
        e = act(lambda: A.activation(rs[:], ps[7][:, 256:512], ACT.Sqrt, bias=eps[:]), R["var", b], R.get(("rn", b - 1)))
        e = dve(lambda: V.reciprocal(rs[:], rs[:]), e)
        e = dve(lambda: V.tensor_tensor(rn[:], ps[7][:, 0:256], rs[:], ALU.mult), e, R.get(("y", b - 1)))
        R["rn", b] = dve(lambda: V.tensor_scalar(rn[:], rn[:], gbt[:, 0:1], gbt[:, 1:2], ALU.mult, ALU.add), e)

    def wout(b):
        ld = sp.dma(lambda: nc.sync.dma_start(xr[:].rearrange("p (c d) -> p c d", c=2), xrv[b]), d_xr, R.get(("base", b - 1)))
        for c in range(2):
            R["y", b] = pe(lambda c=c: mm(ps[7][:, 256 + 128 * c:384 + 128 * c], rn[:, 128 * c:128 * c + 128],
                                          wv[:, 128:256]), R["rn", b])
        R["base", b] = dve(lambda: V.tensor_tensor(ob[0][:], ps[7][:, 256:512], xr[:], ALU.add), R["y", b], ld,
                           R.get(("ost", b - 1)))
        R["ost", b] = act.dma(lambda: nc.scalar.dma_start(ov[b], ob[0][:].rearrange("p (c d) -> p c d", c=2)),
                              d_ob, R["base", b])

    proj(0, 1)
    proj(0, 0)
    stack(0, 1)
    unstack_k(0)
    stack(0, 0)
    unstack_q(0)
    projv(0)
    for b in range(NB):
        more = b + 1 < NB
        score(b, 0)
        score(b, 1)
        if more:
            proj(b + 1, 1)
        for _ in range(0 if b else 4):
            next(disp)
        score(b, 2)
        if b:
            centre(b - 1)
        ktrans(b)
        score(b, 3)
        if more:
            proj(b + 1, 0)
        smat(b)
        if b:
            var(b - 1)
        if staged[0] < EARLY:
            stage()
        score(b, 4)
        av(b, 0)
        score(b, 5)
        if more:
            stack(b + 1, 1)
            unstack_k(b + 1)
        if staged[0] < EARLY:
            stage()
        score(b, 6)
        cross(b)
        if b:
            wout(b - 1)
        score(b, 7)
        if more:
            stack(b + 1, 0)
            unstack_q(b + 1)
        av(b, 1)
        evac(b)
        if more:
            projv(b + 1)
        for _ in range(2):
            if staged[0] < EARLY:
                stage()
        next(disp, None)
        next(disp, None)
    for _ in disp:
        pass
    late = [R["av", NB - 1], R["sc", NB - 1], R["cross", NB - 1], R["p", 8 * NB - 1], state["e"]]
    stage(late)
    centre(NB - 1)
    stage(late)
    var(NB - 1)
    stage(late)
    wout(NB - 1)
    while staged[0] < 40:
        stage(late)
    attn_end = [R["y", NB - 1], R["base", NB - 1], R["rn", NB - 1], R["ost", NB - 1], R["p", 8 * NB - 1], state["e"]]
    e_w3b = act.dma(lambda: nc.scalar.dma_start(
        w3s[:].rearrange("p (e c k) -> p e c k", e=8, c=4)[:, 8 - LATE:8].rearrange("p e c k -> p (e c) k"),
        w3[8 - LATE:8].rearrange("e (c p) k -> p (e c) k", p=128)), d_w3, *late)
    weights = [w_done["v"], w_done["p"], e_w3, e_w3b]

    X = {}
    regs = {}
    W = {}

    def gather(t):
        X["g", t] = pool.dma(lambda: nc.gpsimd.indirect_dma_start(
            xg[t % 4][:], None, xnd, bass.IndirectOffsetOnAxis(ap=gidx[:, t:t + 1], axis=0)),
            d_g[t % 4], X.get(("xT", t - 4)), state["e"], e_st, *attn_end, *(weights if t == 2 else []))

    def xtrans(t):
        X["xT", t] = pe(lambda: T.transpose(ps[5][:, 0:128], xg[t % 4][:], ident[:]), X["g", t], X.get(("xl", t - 1)))
        h = act(lambda: A.copy(xh[t % 2][:], ps[5][:, 0:128]), X["xT", t], X.get(("L1", t - 2)))
        X["xl", t] = dve(lambda: V.tensor_tensor(xl[t % 2][:], ps[5][:, 0:128], xh[t % 2][:], ALU.subtract), h)
        X["sel", t] = dve(lambda: V.tensor_scalar(sel[t % 5][0:64, :], ex[0:64, t:t + 1].to_broadcast([64, 128]),
                                                  pm[0:64, :], None, ALU.is_equal), X.get(("L3", t - 5)), *attn_end, *weights)

    def loadreg(t):
        regs[t] = nc.tensor.value_load(exi[0:1, t:t + 1], min_val=0, max_val=7)

    def layer1(t):
        bank = ps[0]
        n = t % 2

        def rhs(w):
            return w[:, bass.ds(regs[t] * 512, 512)]

        def first():
            if t < 2:
                loadreg(t)
            return mm(bank[:], sel[t % 5][0:64, :], ball[0:64, 0:512], True, False)
        pe(first, X["sel", t], X["xl", t], X.get(("g1", t - 1)), *weights, sig=False)
        pe(lambda: mm(bank[:], xh[n][:], rhs(w1l), False, False), sig=False)
        pe(lambda: mm(bank[:], xl[n][:], rhs(w1h), False, False), sig=False)
        X["L1", t] = pe(lambda: mm(bank[:], xh[n][:], rhs(w1h), False, True))
        X["g1", t] = act(lambda: A.activation(g1[:], bank[:], ACT.Gelu), X["L1", t], X.get(("T1", t - 1)))

    def trans1(t):
        for c in range(4):
            X["T1", t] = pe(lambda c=c: T.transpose(ps[1][:, 128 * c:128 * c + 128], g1[:, 128 * c:128 * c + 128],
                                                    ident[:]), X["g1", t], X.get(("h1l", t - 1)))
        h = act(lambda: A.copy(h1h[:], ps[1][:]), X["T1", t], X.get(("L2", t - 1)))
        X["h1l", t] = dve(lambda: V.tensor_tensor(h1l[:], ps[1][:], h1h[:], ALU.subtract), h, X.get(("L2", t - 1)))

    def layer2(t):
        bank = ps[2]
        n = t % 2

        def rhs(w, c):
            return w[:, bass.ds(regs[t] * 2048 + 512 * c, 512)]
        pe(lambda: mm(bank[:], sel[t % 5][0:64, :], ball[0:64, 512:1024], True, False), X.get(("g2", t - 1)), sig=False)
        for c in range(4):
            cc = slice(128 * c, 128 * c + 128)
            pe(lambda c=c, cc=cc: mm(bank[:], h1h[:, cc], rhs(w2l, c), False, False), X["h1l", t], sig=False)
            pe(lambda c=c, cc=cc: mm(bank[:], h1l[:, cc], rhs(w2h, c), False, False), sig=False)
            X["L2", t] = pe(lambda c=c, cc=cc: mm(bank[:], h1h[:, cc], rhs(w2h, c), False, c == 3))
            if c == 1 and t + 2 < NT:
                pe(lambda: loadreg(t + 2), sig=False)
        X["g2", t] = act(lambda: A.activation(g2[:], bank[:], ACT.Gelu), X["L2", t], X.get(("T2", t - 1)))

    def trans2(t):
        for c in range(4):
            X["T2", t] = pe(lambda c=c: T.transpose(ps[3][:, 128 * c:128 * c + 128], g2[:, 128 * c:128 * c + 128],
                                                    ident[:]), X["g2", t], X.get(("h2", t - 1)))
        X["h2", t] = dve(lambda: V.tensor_copy(h2t[t % 2][:], ps[3][:]), X["T2", t], X.get(("L3", t - 2)))

    def layer3(t):
        bank = ps[4][:, 0:128]
        n = t % 2

        def rhs(c):
            return w3s[:, bass.ds(regs[t] * 512 + 128 * c, 128)]
        pe(lambda: mm(bank, sel[t % 5][0:64, :], ball[0:64, 1024:1152], True, False), X.get(("ys", t - 1)), sig=False)
        for c in range(4):
            X["L3", t] = pe(lambda c=c: mm(bank, h2t[n][:, 128 * c:128 * c + 128], rhs(c), False, c == 3), X["h2", t])
        X["ys", t] = dve(lambda: V.tensor_scalar(ys[n][:], bank, 0.5, None, ALU.mult), X["L3", t], X.get(("add", t - 2)))

    def scatter(t):
        X["add", t] = pool.dma(lambda: nc.gpsimd.indirect_dma_start(
            out, bass.IndirectOffsetOnAxis(ap=sidx[:, t:t + 1], axis=0), ys[t % 2][:], None,
            bounds_check=NTOK - 1, oob_is_err=False, compute_op=ALU.add),
            d_s, X["ys", t], X.get(("add", t - 1)), *attn_end)

    gather(0)
    gather(1)
    xtrans(0)
    layer1(0)
    gather(2)
    gather(3)
    xtrans(1)
    trans1(0)
    layer1(1)
    xtrans(2)
    for t in range(NT):
        if t + 4 < NT:
            gather(t + 4)
        layer2(t)
        if t + 1 < NT:
            trans1(t + 1)
        if t + 3 < NT:
            xtrans(t + 3)
        if t + 2 < NT:
            layer1(t + 2)
        trans2(t)
        if t:
            layer3(t - 1)
            scatter(t - 1)
    layer3(NT - 1)
    scatter(NT - 1)
    pool.ops.append((lambda: None, [X["add", NT - 1]], False))

    with nc.Block() as block:
        @block.sync
        def _(eng):
            sp.emit(eng)

        @block.scalar
        def _(eng):
            act.emit(eng)

        @block.vector
        def _(eng):
            dve.emit(eng)

        @block.gpsimd
        def _(eng):
            pool.emit(eng)

        @block.tensor
        def _(eng):
            pe.emit(eng)


def kernel(**inputs):
    import concourse.bacc as bacc
    from concourse.bass_utils import run_bass_kernel_spmd

    a = {k: np.asarray(v) for k, v in inputs.items()}
    swap = np.arange(128) ^ 1
    wqT = a["L0_attn_WQ"].reshape(128, 128).T
    wkT = a["L0_attn_WK"].reshape(128, 128).T
    wvT = a["L0_attn_WV"].reshape(128, 128).T
    cf, cb = constants()
    arrays = {
        "x": a["L0_attn_x"].reshape(NTOK, D),
        "wqkv": np.concatenate([wqT, wqT[:, swap], wkT, wkT[:, swap]], axis=1),
        "wvo": np.concatenate([wvT, a["L0_attn_WO"]], axis=1),
        "gb": np.stack([a["L0_attn_gamma"], a["L0_attn_beta"]], axis=1),
        "etokT": a["L0_ffn_expert_tokens"].T,
        "w1": a["L0_ffn_W1"], "w2": a["L0_ffn_W2"], "w3": a["L0_ffn_W3"],
        "bias": np.concatenate([a["L0_ffn_b1"], a["L0_ffn_b2"], a["L0_ffn_b3"]], axis=1),
        "cf": cf, "cb": cb,
    }
    arrays = {k: np.ascontiguousarray(v) for k, v in arrays.items()}
    nc = bacc.Bacc("TRN2", target_bir_lowering=False, num_devices=1)
    aps = {k: nc.dram_tensor(f"in_{k}", v.shape, mybir.dt.from_np(v.dtype), kind="ExternalInput").ap()
           for k, v in arrays.items()}
    out = nc.dram_tensor("out_0", (NTOK, D), F32, kind="ExternalOutput").ap()
    moe_retention_kernel(nc, *aps.values(), out)
    r = run_bass_kernel_spmd(nc, [{f"in_{k}": v for k, v in arrays.items()}], core_ids=[0])
    return r.results[0]["out_0"].reshape(8, 256, 128)
```

```python
import numpy as np
import concourse.bass as bass
from concourse import mybir

F32 = mybir.dt.float32
F32R = mybir.dt.float32r
BF16 = mybir.dt.bfloat16
I32 = mybir.dt.int32
U32 = mybir.dt.uint32
ALU = mybir.AluOpType
ACT = mybir.ActivationFunctionType
AX = mybir.AxisListType

NTOK, D, HID, NEXP = 2048, 128, 512, 8
NB, SEQ, NHEAD = 8, 256, 16
NT = 39
NTP = 40
LATE = 3

C_ID, C_MASK, C_BLK, C_CEN = 0, 128, 256, 384
C_TAB = 512
C_P = 1536
C_IT = 1537
C_K = 1577
C_L = 1593
C_G = 1657
C_REP = 1661
C_N = 2173
B_IO, B_TRI, B_ONE, B_LM = 0, 128, 256, 384
B_N = 448


def constants():
    c = np.zeros((128, C_N), np.float32)
    p = np.arange(128)
    c[:, C_ID:C_ID + 128] = np.eye(128)
    c[:, C_MASK:C_MASK + 128] = p[None, :] >= p[:, None]
    same = (p[:, None] // 8) == (p[None, :] // 8)
    c[:, C_BLK:C_BLK + 128] = same
    c[:, C_CEN:C_CEN + 128] = np.eye(128) - same / 8.0
    ex = np.arange(0, 8, 2, dtype=np.float32) / np.float32(8)
    angle = np.power(np.float32(10.0), np.float32(-4.0) * ex).astype(np.float32)
    pos = np.arange(SEQ, dtype=np.float32)
    ang = (pos[None, :] * angle[(p % 8) // 2][:, None]).astype(np.float32).astype(np.float64)
    sgn = np.where(p % 2 == 0, -1.0, 1.0)[:, None]
    g = (1.0 - 2.0 ** (-5.0 - (p // 8)))[:, None]
    up, down = g ** pos[None, :], g ** -pos[None, :].astype(np.float64)
    for n, t in enumerate((np.cos(ang) * up, np.sin(ang) * sgn * up, np.cos(ang) * down, np.sin(ang) * sgn * down)):
        c[:, C_TAB + 256 * n:C_TAB + 256 * (n + 1)] = t
    c[:, C_P] = p
    c[:, C_IT:C_IT + NTP] = np.arange(NTP)
    c[:, C_K:C_K + 16] = 128 * np.arange(16)
    c[:, C_G:C_G + 4] = (p[:, None] // 32) == np.arange(4)[None, :]
    e = np.arange(8)
    c[:, C_L:C_L + 64] = (e[None, :] < e[:, None]).reshape(1, 64)
    m, part, u = p // 32, (p // 8) % 4, p % 8
    for n, use in enumerate((part < 2, part >= 2, part % 2 == 0, part % 2 == 1)):
        c[:, C_REP + 128 * n:C_REP + 128 * (n + 1)] = ((p[:, None] % 32) == (8 * m + u)[None, :]) & use[None, :]
    b = np.zeros((128, B_N), np.float32)
    b[:, B_IO:B_IO + 128] = p[None, :]
    b[:, B_TRI:B_TRI + 128] = p[:, None] < p[None, :]
    b[:, B_ONE:B_ONE + 128] = 1
    b[:, B_LM:B_LM + 64] = (e[None, :] < e[:, None]).reshape(1, 64)
    return c, b


class Queue:

    def __init__(self, sem):
        self.sem, self.n, self.ops = sem, 0, []

    def __call__(self, fn, *needs, sig=True):
        self.ops.append((fn, [x for x in needs if x is not None], sig))
        if sig:
            self.n += 1
            return (self.sem, self.n)

    def dma(self, fn, done, *needs):
        self.ops.append((fn, [x for x in needs if x is not None], done.sem))
        done.n += 16
        return (done.sem, done.n)

    def emit(self, eng):
        seen = {}
        for fn, needs, sig in self.ops:
            for sem, value in (x for n in needs for x in (n if isinstance(n, list) else [n])):
                if seen.get(sem.name, 0) < value:
                    eng.wait_ge(sem, value)
                    seen[sem.name] = value
            ins = fn()
            if sig is True:
                ins.then_inc(self.sem, 1)
            elif sig is not False:
                ins.then_inc(sig, 16)


class DmaSem:
    def __init__(self, sem):
        self.sem, self.n = sem, 0


def moe_retention_kernel(nc, x, wqkv, wvo, gb, etokT, w1, w2, w3, b1t, b23, cf, cb, out):
    def at(name, cols, dt, off, parts=128):
        return nc.alloc_sbuf_tensor_at(name, [parts, cols], dt, offset=off)

    R0 = 16512
    W2H, W2L = R0, R0 + 65536
    W1O, W3O = R0 + 131072, R0 + 147456
    B2O, B3O = R0 + 163840, R0 + 180224
    F0 = R0 + 184320
    w2h = at("w2h", 8 * 2048, F32R, W2H)
    w2l = at("w2l", 8 * 2048, F32R, W2L)
    w1s = at("w1s", 8 * 512, F32, W1O)
    w3s = at("w3s", 8 * 512, F32, W3O)
    b2s = at("b2s", 8 * 512, F32, B2O)
    b3s = at("b3s", 8 * 128, F32, B3O)
    o = F0
    ident = at("ident", 128, F32, o); o += 512
    gidx = at("gidx", NTP, U32, o); o += 160
    sidx = at("sidx", NTP, U32, o); o += 160
    ex = at("ex", NTP, F32, o); o += 160
    exi = at("exi", NTP, I32, o); o += 160
    b1s = at("b1s", 32, F32, o); o += 128
    stg = [at(f"stg{i}", 512, F32, o + 2048 * i) for i in range(4)]; o += 8192
    G0 = o
    xg = [at(f"xg{i}", 128, F32, o + p) for i, p in enumerate((1536, 512, 1024, 0))]; o += 2048
    xf = [at(f"xf{i}", 128, F32, o + 512 * i) for i in range(2)]; o += 1024
    w1c = at("w1c", 512, F32, o); o += 2048
    g1 = at("g1", 512, F32, o); o += 2048
    h1h = at("h1h", 512, F32R, o); o += 2048
    h1l = at("h1l", 512, F32R, o); o += 2048
    g2 = at("g2", 512, F32, o); o += 2048
    h2t = [at(f"h2t{i}", 512, F32, o + 2048 * i) for i in range(2)]; o += 4096
    ys = [at(f"ys{i}", 128, F32, o + 512 * i) for i in range(2)]; o += 1024
    assert o <= 229368
    o = G0
    cs = at("cs", 384, F32, o); o += 1536
    small = at("small", C_REP - C_P, F32, o); o += 512
    cbs = at("cbs", B_N, BF16, o); o += 896
    wq = at("wq", 512, F32, o); o += 2048
    et = at("et", 8, F32, o); o += 32
    mv = at("mv", 32, F32, o); o += 128
    st = at("st", 96, F32, o); o += 384
    vs = at("vs", 128, F32, o); o += 512
    qr = [at("qr0", 256, F32, o), at("qr1", 256, F32, o + 1024)]; o += 2048
    kr = [at("kr0", 256, F32, o), at("kr1", 256, F32, o + 1024)]; o += 2048
    qh = at("qh", 256, F32R, o); o += 1024
    rstd = at("rstd", 16, F32, o); o += 64
    o += 32
    wv = at("wv", 256, F32, o); o += 1024
    gbt = at("gbt", 2, F32, o); o += 32
    xr = [at(f"xr{i}", 256, F32, o + 1024 * i) for i in range(2)]; o += 2048
    rt = at("rt", 256, F32, o); o += 1024
    sq = at("sq", 256, F32, o); o += 1024
    rn = at("rn", 256, F32, o); o += 1024
    ob = at("ob", 256, F32, o); o += 1024
    vr = at("vr", 32, F32, o); o += 128
    eps = at("eps", 1, F32, o); o += 32
    nb = at("nb", 16, F32, o); o += 64
    assert o <= 229368, o
    A0 = W2H + 40960
    B0 = W2L + 40960
    C0, D0, E0 = W3O + 10240, B2O, W1O + 10240
    o = A0
    oh = [at(f"oh{i}", 128, BF16, o + 256 * i) for i in range(8)]; o += 2048
    bt = at("bt", 16 * NTP, BF16, o); o += 1280
    s1 = at("s1", 128, F32, A0)
    cm = at("cm", 128, F32, A0 + 512)
    past = at("past", 7 * NTP, F32, A0)
    sc = at("sc", 128, F32, A0 + 1024)
    s0 = at("s0", 128, F32, A0 + 1536)
    msk = at("msk", 128, BF16, A0 + 2048)
    ne = at("ne", 8, F32, A0 + 2304)
    ce = at("ce", 8, F32, A0 + 2336)
    be = at("be", 8, F32, A0 + 2368)
    dst = at("dst", 32, F32, A0 + 2400)
    dsi = at("dsi", 32, I32, A0 + 2528)
    dhi = at("dhi", 32, I32, A0 + 2656)
    dlo = at("dlo", 32, I32, A0 + 2784)
    dtf = at("dtf", 32, F32, o); o += 128
    dpf = at("dpf", 32, F32, o); o += 128
    tbh = at("tbh", 2 * NTP, F32, o); o += 320
    tbg = at("tbg", NTP, F32, o); o += 160
    tbe = at("tbe", NTP, F32, o - 480 - 256)
    assert o <= A0 + 4096
    xnt = at("xnt", 2048, F32, A0 + 4096)
    pt = [at(f"pt{i}", 512, F32, A0 + 12288 + 2048 * i) for i in range(6)]
    qx = at("qx", 4096, F32R, B0)
    xn = at("xn", 2048, F32, A0 + 12288)
    kst = [at(f"kst{i}", 1024, F32R, B0 + 16384 + 4096 * i) for i in range(2)]
    gt = at("gt", 1024, BF16, W1O)
    eq = at("eq", 1024, BF16, W1O + 2048)
    vm = [at(f"vm{i}", 640, F32, C0 + 2560 * i) for i in range(2)]
    kt = at("kt", 128, F32, C0 + 5120)
    smt = at("smt", 128, F32, C0 + 5632)
    tab = at("tab", 1024, F32, D0)
    tmp = at("tmp", 512, F32, E0)
    tmp2 = at("tmp2", B_N, F32, A0 + 1536)
    repf = at("repf", 512, F32, A0 + 12288 + 10240)
    repm = at("repm", 2048, F32R, D0 + 4096)
    ql = at("ql", 256, F32R, E0 + 2048)
    kh = at("kh", 256, F32R, E0 + 4096)
    kl = at("kl", 256, F32R, E0 + 5120)
    ps = [nc.alloc_psum_tensor(f"ps{i}", [128, 512], F32) for i in range(8)]
    xnd = nc.dram_tensor("xnd", (NTOK, D), F32, kind="Internal").ap()

    cmask, cblk, ccen = (cs[:, 128 * i:128 * i + 128] for i in range(3))
    pcol = small[:, C_P - C_P:C_P - C_P + 1]
    iot = small[:, C_IT - C_P:C_IT - C_P + NTP]
    grp = lambda g: small[:, C_G - C_P + g:C_G - C_P + g + 1]
    k128 = small[:, C_K - C_P:C_K - C_P + 16]
    lm8 = small[:, C_L - C_P:C_L - C_P + 64]
    b_io, b_tri, b_one = (cbs[:, 128 * i:128 * i + 128] for i in range(3))
    b_lm = cbs[:, B_LM:B_LM + 64]

    S = lambda name: nc.alloc_semaphore(name)
    pe, act, dve, pool, sp = (Queue(S(f"q_{n}")) for n in ("pe", "act", "dve", "pool", "sp"))
    d_const, d_xn = DmaSem(S("d_const")), DmaSem(S("d_xn"))
    d_bias, d_w1, d_w3, d_b2 = DmaSem(S("d_bias")), DmaSem(S("d_w1")), DmaSem(S("d_w3")), DmaSem(S("d_b2"))
    d_xr = [DmaSem(S(f"d_xr{i}")) for i in range(2)]
    d_stg = [DmaSem(S(f"d_stg{i}")) for i in range(4)]
    d_g = [DmaSem(S(f"d_g{i}")) for i in range(4)]
    d_s = DmaSem(S("d_s"))
    V, A, G, T = nc.vector, nc.scalar, nc.gpsimd, nc.tensor

    r3 = lambda ap, a, b: ap.rearrange("p (a b) -> p a b", a=a, b=b)

    xt = x.rearrange("(t p) d -> p t d", p=128)
    xv = xn[:].rearrange("p (t d) -> p t d", d=128)
    d_x4 = [DmaSem(S(f"d_x{i}")) for i in range(4)]
    e_x = []
    for i in range(4):
        e_x.append(sp.dma(lambda i=i: nc.sync.dma_start(xv[:, 4 * i:4 * i + 4, :], xt[:, 4 * i:4 * i + 4, :]), d_x4[i]))
    d_rep, d_id, d_w = DmaSem(S("d_rep")), DmaSem(S("d_id")), DmaSem(S("d_w"))
    on_act = lambda done, dst_, src_: act.dma(lambda: nc.scalar.dma_start(dst_, src_), done)
    on_sp = lambda done, dst_, src_: sp.dma(lambda: nc.sync.dma_start(dst_, src_), done)
    on_act(d_rep, small[:], cf[:, C_P:C_REP])
    e_r = on_act(d_rep, repf[:], cf[:, C_REP:C_N])
    e_id = on_act(d_id, ident[:], cf[:, 0:128])
    on_act(d_w, wq[:], wqkv)
    e_w = on_act(d_w, tab[:], cf[:, C_TAB:C_TAB + 1024])
    for dst_, src_ in ((et[:], etokT), (wv[:], wvo), (tmp2[:], cb), (cs[:], cf[:, 128:512])):
        on_sp(d_const, dst_, src_)
    e_c = on_sp(d_const, gbt[:], gb)
    on_sp(d_bias, b1s[:], b1t)
    e_b = on_sp(d_bias, b3s[:], b23[:, 4096:5120].partition_broadcast(128))
    for c in range(2):
        e_vz = pool(lambda c=c: G.memset(vm[c][:], 0.0))
    e_qz = pool(lambda: G.memset(qx[:].bitcast(F32), 0.0))

    def load1(es, *needs):
        return act.dma(lambda: nc.scalar.dma_start(w1s[:].rearrange("p (e k) -> p e k", e=8)[:, es],
                                                   w1[es].rearrange("e p k -> p e k")), d_w1, *needs)

    def load3(es, *needs):
        return act.dma(lambda: nc.scalar.dma_start(
            w3s[:].rearrange("p (e c k) -> p e c k", e=8, c=4)[:, es].rearrange("p e c k -> p (e c) k"),
            w3[es].rearrange("e (c p) k -> p (e c) k", p=128)), d_w3, *needs)

    w2src = w2.rearrange("e (c p) k -> e c p k", p=128)
    pieces = []
    for e in range(8):
        for c in range(4):
            pieces.append((w2src[e, c], w2h[:, e * 2048 + c * 512:][:, 0:512], w2l[:, e * 2048 + c * 512:][:, 0:512]))
    last_lo = [None] * 4
    highs, lows = {}, {}

    EARLY = 4 * (8 - LATE)
    RING = EARLY + 4
    d_raw = [DmaSem(S(f"d_raw{i}")) for i in range(4)]

    def load(i):
        loaded.append(sp.dma(lambda: nc.sync.dma_start(stg[i % 4][:], pieces[i][0]), d_stg[i % 4], last_lo[i % 4]))

    def high_part(i, *needs, on=None):
        src, hi, lo = pieces[i]
        raw = stg[i % 4][:] if i < RING else lo.bitcast(F32)
        eng, copy = on or (act, A.copy)
        highs[i] = eng(lambda: copy(hi, raw), loaded[i], *needs)

    def low_part(i, *needs, on=None):
        src, hi, lo = pieces[i]
        raw = stg[i % 4][:] if i < RING else lo.bitcast(F32)
        eng, sub = on or (dve, V.tensor_tensor)
        lows[i] = eng(lambda: sub(lo, raw, hi, ALU.subtract), highs[i], *needs)
        if i < RING:
            last_lo[i % 4] = lows[i]

    def stage(n_high, n_low):
        for _ in range(n_high):
            if len(highs) < EARLY:
                high_part(len(highs))
        for _ in range(n_low):
            i = len(lows)
            if i < EARLY:
                low_part(i, on=(pool, G.tensor_tensor))
                if i + 4 < RING:
                    load(i + 4)

    def load_raw(*needs):
        for j in range(4):
            e, c = divmod(RING + 2 * j, 4)
            dst = w2l[:, e * 2048 + c * 512:][:, 0:1024].bitcast(F32)
            loaded.extend(2 * [sp.dma(lambda e=e, c=c, dst=dst: nc.sync.dma_start(
                r3(dst, 2, 512), w2src[e, c:c + 2].rearrange("c p k -> p c k")), d_raw[j], *needs)])

    loaded = []

    dve(lambda: V.memset(eps[:], 1e-5))
    mvv = mv[:].rearrange("p (t k) -> p t k", k=2)
    psd = ps[6][:, 256:392]
    e_sd, e_xn, e_xt = [], [], []

    def stats(g):
        for t in range(4 * g, 4 * g + 4):
            e = dve(lambda t=t: V.bn_stats(st[:, 6 * t:6 * t + 6], xn[:, 128 * t:128 * t + 128]), e_x[g])
        for t in range(4 * g, 4 * g + 4):
            e = dve(lambda t=t: V.bn_aggr(mv[:, 2 * t:2 * t + 2], st[:, 6 * t:6 * t + 6]), e)
        e_sd.append(act(lambda: A.activation(rstd[:, 4 * g:4 * g + 4], mvv[:, 4 * g:4 * g + 4, 1], ACT.Sqrt,
                                             bias=eps[:]), e))

    def normalise(g):
        gs = slice(4 * g, 4 * g + 4)
        e = dve(lambda: V.reciprocal(rstd[:, gs], rstd[:, gs]), e_sd[g])
        e_nb = dve(lambda: V.scalar_tensor_tensor(nb[:, gs], mvv[:, gs, 0], -1.0, rstd[:, gs], ALU.mult, ALU.mult), e)
        for t in range(4 * g, 4 * g + 4):
            c = slice(128 * t, 128 * t + 128)
            if t % 2:
                e_xn.append(act(lambda t=t, c=c: A.activation(xn[:, c], xn[:, c], ACT.Identity, bias=nb[:, t:t + 1],
                                                              scale=rstd[:, t:t + 1]), e_nb))
            else:
                e_xn.append(dve(lambda t=t, c=c: V.tensor_scalar(xn[:, c], xn[:, c], mv[:, 2 * t:2 * t + 1],
                                                                 rstd[:, t:t + 1], ALU.subtract, ALU.mult), e))

    def transpose_x(g):
        bank = ps[(3, 4, 7, 2)[g]]
        for t in range(4 * g, 4 * g + 4):
            e = pe(lambda t=t: T.transpose(bank[:, 128 * (t % 4):128 * (t % 4) + 128],
                                           xn[:, 128 * t:128 * t + 128], ident[:]), e_xn[t], e_id)
        e_xt.append(act(lambda: A.copy(xnt[:, 512 * g:512 * g + 512], bank[:]), e))

    def expert_scores(g):
        for t in range(4 * g, 4 * g + 4):
            e = pe(lambda t=t: T.matmul(psd[:, 8 * t:8 * t + 8], xnt[:, 128 * t:128 * t + 128], et[:],
                                        start=True, stop=True, skip_group_check=True), e_xt[g], e_c)
        return e

    def rep_groups(gs, eng, mul):
        for g in gs:
            e = eng(lambda g=g: mul(r3(repm[:], 4, 512)[:, :, 128 * g:128 * g + 128], r3(repf[:], 4, 128), grp(g)), e_r)
        return e

    def halve_bias():
        return pool(lambda: G.tensor_scalar(b3s[:], b3s[:], 0.5, None, ALU.mult), e_b)

    state = {}

    def dispatch():
        def step(fn, *needs):
            state["e"] = dve(fn, state.get("e"), *needs)
        scv = r3(sc[:], 16, 8)
        s_oth = scv.unsqueeze(2).to_broadcast([128, 16, 8, 8])
        s_own = scv.unsqueeze(3).to_broadcast([128, 16, 8, 8])
        four = lambda a: a.rearrange("p (t e f) -> p t e f", t=16, e=8)
        step(lambda: V.tensor_copy(sc[:], psd[:, 0:128]), e_sc)
        step(lambda: V.tensor_tensor(four(gt[:]), s_oth, s_own, ALU.is_gt))
        yield
        step(lambda: V.tensor_tensor(four(eq[:]), s_oth, s_own, ALU.is_equal))
        step(lambda: V.tensor_tensor(r3(eq[:], 16, 64), r3(eq[:], 16, 64),
                                     b_lm.unsqueeze(1).to_broadcast([128, 16, 64]), ALU.mult), e_cb)
        yield
        step(lambda: V.tensor_tensor(gt[:], gt[:], eq[:], ALU.add))
        step(lambda: V.tensor_reduce(s0[:], r3(gt[:], 128, 8), AX.X, ALU.add))
        R["gt"] = state["e"]
        step(lambda: V.tensor_scalar(msk[:], s0[:], 2.0, None, ALU.is_lt))
        yield
        e_m = state["e"]
        mv3 = r3(msk[:], 16, 8)
        pe(lambda: T.matmul(psd[:, 0:128], b_tri, msk[:], start=True, stop=False, skip_group_check=True), e_m, sig=False)
        for t in range(16):
            e_p = pe(lambda t=t: T.matmul(
                r3(psd[:, 8 * (t + 1):136], 16 - t, 8), b_one,
                mv3[:, t:t + 1, :].to_broadcast([128, 16 - t, 8]), start=False, stop=(t == 15), skip_group_check=True))
        yield
        step(lambda: V.tensor_copy(ne[:], psd[:, 128:136]), e_p)
        step(lambda: V.tensor_tensor(r3(cm[:], 8, 16), ne[:].unsqueeze(2).to_broadcast([128, 8, 16]),
                                     k128.unsqueeze(1).to_broadcast([128, 8, 16]), ALU.is_gt))
        step(lambda: V.tensor_reduce(ce[:], r3(cm[:], 8, 16), AX.X, ALU.add))
        step(lambda: V.tensor_tensor(r3(cm[:, 0:64], 8, 8), ce[:].unsqueeze(1).to_broadcast([128, 8, 8]),
                                     r3(lm8, 8, 8), ALU.mult))
        step(lambda: V.tensor_reduce(be[:], r3(cm[:, 0:64], 8, 8), AX.X, ALU.add))
        step(lambda: V.scalar_tensor_tensor(r3(s0[:], 16, 8), be[:].unsqueeze(1).to_broadcast([128, 16, 8]), 128.0,
                                            r3(psd[:, 0:128], 16, 8), ALU.mult, ALU.add))
        R["psd"] = state["e"]
        yield
        step(lambda: V.scalar_tensor_tensor(s1[:], s0[:], 1.0, msk[:], ALU.add, ALU.mult))
        step(lambda: V.tensor_reduce(dst[:, 0:16], r3(s1[:], 16, 8), AX.X, ALU.max))
        step(lambda: V.tensor_scalar(dst[:, 0:16], dst[:, 0:16], -1.0, None, ALU.add))
        yield
        step(lambda: V.scalar_tensor_tensor(s1[:], s0[:], -8192.0, msk[:], ALU.add, ALU.mult))
        step(lambda: V.tensor_reduce(dst[:, 16:32], r3(s1[:], 16, 8), AX.X, ALU.min))
        step(lambda: V.tensor_scalar(dst[:, 16:32], dst[:, 16:32], 8192.0, None, ALU.add))
        step(lambda: V.tensor_copy(dsi[:], dst[:]))
        step(lambda: V.tensor_scalar(dhi[:], dsi[:], 7, None, ALU.logical_shift_right))
        step(lambda: V.tensor_scalar(dlo[:], dsi[:], 127, None, ALU.bitwise_and))
        step(lambda: V.tensor_copy(dtf[:], dhi[:]))
        step(lambda: V.tensor_copy(dpf[:], dlo[:]))
        yield
        step(lambda: V.tensor_tensor(r3(past[:], NTP, 7), iot.unsqueeze(2).to_broadcast([128, NTP, 7]),
                                     be[:, 1:8].unsqueeze(1).to_broadcast([128, NTP, 7]), ALU.is_ge))
        step(lambda: V.tensor_reduce(ex[:], r3(past[:], NTP, 7), AX.X, ALU.add))
        step(lambda: V.tensor_copy(exi[:], ex[:]))
        yield
        e0, used = state["e"], None
        bt3 = bt[:].rearrange("p (i k c) -> p i k c", i=8, k=2)
        for j in range(4):
            i8 = slice(8 * j, 8 * j + 8)
            for i in range(8 * j + 4, 8 * j + 8):
                e_oh = pool(lambda i=i: G.tensor_scalar(oh[i % 8][:], b_io, dpf[:, i:i + 1], None, ALU.is_equal),
                            used, e0)
            yield
            t1 = iot[:, 8 * (j % 2) + 1:8 * (j % 2) + 9]
            e = dve(lambda i8=i8: V.tensor_tensor(bt3[:, :, 1, :], iot.unsqueeze(1).to_broadcast([128, 8, NTP]),
                                                  dtf[:, i8].unsqueeze(2).to_broadcast([128, 8, NTP]), ALU.is_equal),
                    e0, used)
            dve(lambda t1=t1: V.tensor_tensor(bt3[:, :, 0, :], bt3[:, :, 1, :],
                                              t1.unsqueeze(2).to_broadcast([128, 8, NTP]), ALU.mult), e)
            e = dve(lambda: V.tensor_scalar(bt3[:, :, 1, :], bt3[:, :, 1, :], pcol, None, ALU.mult), e)
            yield
            for i in range(8 * j, 8 * j + 4):
                e = dve(lambda i=i: V.tensor_scalar(oh[i % 8][:], b_io, dpf[:, i:i + 1], None, ALU.is_equal), used)
            yield
            for i in range(8 * j, 8 * j + 8):
                used = pe(lambda i=i: T.matmul(r3(psd[:, 0:2 * NTP], 2, NTP), oh[i % 8][:], bt3[:, i % 8],
                                               start=(i % 8 == 0), stop=(i % 8 == 7),
                                               skip_group_check=True), e, e_oh, R.get("rt"))
            if j == 0:
                R["psd"] = dve(lambda: V.tensor_copy(tbh[:], psd[:, 0:2 * NTP]), used)
            else:
                R["psd"] = dve(lambda: V.tensor_tensor(tbh[:], tbh[:], psd[:, 0:2 * NTP], ALU.add), used, R["psd"])
            yield
        state["e"] = R["psd"]
        step(lambda: V.tensor_scalar(tbg[:], tbh[:, 0:NTP], -1.0, 0.0, ALU.add, ALU.max))
        step(lambda: V.scalar_tensor_tensor(tbg[:], tbg[:], 128.0, tbh[:, NTP:2 * NTP], ALU.mult, ALU.add))
        step(lambda: V.tensor_copy(gidx[:], tbg[:]))
        step(lambda: V.tensor_scalar(tbe[:], tbh[:, 0:NTP], 0.0, 4096.0, ALU.is_equal, ALU.mult))
        step(lambda: V.tensor_tensor(tbe[:], tbe[:], tbg[:], ALU.add))
        step(lambda: V.tensor_copy(sidx[:], tbe[:]))
        yield

    disp = dispatch()

    ov = out.rearrange("(b c p) d -> b p c d", p=128, c=2)
    xrv = x.rearrange("(b c p) d -> b p c d", p=128, c=2)
    mm = lambda o_, l, r, s=True, p=True: T.matmul(o_, l, r, start=s, stop=p, skip_group_check=True)
    R = {}
    d_ob = DmaSem(S("d_ob"))
    tabv = {0: tab[:, 0:512], 1: tab[:, 512:1024]}

    def proj(b, n):
        xs = xnt[:, 256 * b:256 * b + 256]
        for k in range(2):
            R["proj", n, b] = pe(lambda k=k: mm(ps[n][:, 256 * k:256 * k + 256], wq[:, 256 * n + 128 * k:256 * n + 128 * k + 128], xs),
                   R.get(("qx", 0, b - 1)) if n == 0 else R.get(("kst", 0, b - 1)), e_xt[b // 2], e_w)

    def rotate(b, n):
        dstb = (qr, kr)[n][b % 2]
        hi, lo = ((qh, ql), (kh, kl))[n]
        e = dve(lambda: V.tensor_tensor(tmp[:], ps[n][:], tabv[n], ALU.mult), R["proj", n, b], e_w, R.get("tmp"))
        R["tmp"] = R["rot", n, b] = dve(lambda: V.tensor_tensor(dstb[:], tmp[:, 0:256], tmp[:, 256:512], ALU.add), e,
                                        R.get(("cross", b - 2)), R.get(("kt", b - 2)))
        e = act(lambda: A.copy(hi[:], dstb[:]), R["tmp"], R.get(("rep", n, b - 1)))
        R["lo", n, b] = pool(lambda: G.tensor_tensor(lo[:], dstb[:], hi[:], ALU.subtract), e, R.get(("rep", n, b - 1)))

    def stack(b, n):
        hi, lo = ((qh, ql), (kh, kl))[n]
        bank = ((ps[0], ps[5]), (ps[1], ps[0]))[n]
        free = (R["kst", 1, b], R.get(("qx", 1, b - 1))) if n == 0 else (R["rot", 1, b], R["rot", 0, b])
        for g in range(4):
            cols = slice(256 * (g // 2), 256 * (g // 2) + 256)
            for k, (src, s_) in enumerate(((hi, True), (lo, False))):
                w = repm[:, 1024 * n + 512 * k + 128 * g:1024 * n + 512 * k + 128 * g + 128]
                e = pe(lambda g=g, src=src, s_=s_, w=w, cols=cols: mm(bank[g % 2][:, cols], w, src[:], s_, not s_),
                       R["lo", n, b], free[g % 2], e_rep)
            R["rep", n, g, b] = R["rep", n, b] = e

    def unstack_k(b):
        for i, bank, eng, copy in ((0, ps[1], act, A.copy), (1, ps[0], dve, V.tensor_copy)):
            R["kst", i, b] = eng(lambda i=i, bank=bank, copy=copy: copy(
                kst[b % 2][:].rearrange("p (j i c) -> p j i c", j=2, i=2)[:, :, i, :], r3(bank[:], 2, 256)),
                                 R["rep", 1, 2 + i, b], R.get(("sc", b - 2)))

    def unstack_q(b, i):
        qv = qx[:].rearrange("p (j i m c) -> p j i m c", j=2, i=2, m=4)
        R["qx", i, b] = []
        for eng, copy, ms in ((act, A.copy, (0, 1)), (dve, V.tensor_copy, (2, 3))):
            for m in ms:
                rows = slice(32 * m, 32 * m + 32)
                e = eng(lambda m=m, rows=rows, copy=copy: copy(
                    qv[rows, :, i, m, :], r3(ps[(0, 5)[i]][rows, :], 2, 256)),
                    R["rep", 0, 2 + i, b], R.get(("sc", b - 1)), e_qz)
            R["qx", i, b].append(e)

    def projv(b):
        for c in range(2):
            R["v", b] = pe(lambda c=c: mm(ps[2][:, 128 * c:128 * c + 128],
                                          xnt[:, 256 * b + 128 * c:256 * b + 128 * c + 128], wv[:, 0:128]),
                           R.get(("smt", b - 1)), R.get(("vm", b - 1)), e_xt[3], e_c)

    def unpackv(b):
        for c in range(2):
            R["vm", b] = act(lambda c=c: A.copy(
                vm[c][:].rearrange("p (g m u) -> p g m u", g=4, m=4)[:, :, :, 0:8],
                ps[2][:, 128 * c:128 * c + 128].rearrange("p (g m u) -> p g m u", g=4, m=4)),
                R["v", b], R.get(("av", b - 1)), e_vz)
        R["vs", b] = act(lambda: A.copy(vs[:], ps[2][:, 0:128]), R["v", b], R.get(("s", b - 1)))

    def ktrans(b):
        e = pe(lambda: T.transpose(ps[2][:, 256:384], kr[b % 2][:, 0:128], ident[:]), R["rot", 1, b], R["vs", b])
        R["kt", b] = act(lambda: A.copy(kt[:], ps[2][:, 256:384]), e, R.get(("s", b - 1)))

    def smat(b):
        R["s", b] = pe(lambda: mm(ps[2][:, 384:512], kt[:], vs[:]), R["kt", b])
        R["smt", b] = dve(lambda: V.tensor_tensor(smt[:], ps[2][:, 384:512], cblk, ALU.mult), R["s", b],
                          R.get(("cross", b - 1)))

    def score(b, i):
        c, g = divmod(i, 4)
        n = 8 * b + i
        bank, p = 3 + n % 2, pt[n % 6]
        qv = qx[:].rearrange("p (g m c i) -> p g m c i", g=4, m=4, c=2)
        R["sc", b] = pe(lambda: mm(r3(ps[bank][:], 4, 128), kst[b % 2][:, 256 * g + 128 * c:256 * g + 128 * c + 128],
                                   qv[:, g, :, c, :]),
                        R["qx", g % 2, b], R["kst", g % 2, b], R.get(("evac", n - 2)), e_xt[n % 2])
        if i in (1, 2, 7):
            e = R["evac", n] = act(lambda: A.copy(p[:], ps[bank][:]), R["sc", b], R.get(("avn", n - 6)), e_rep, e_st, e_c)
            R["p", n] = pool(lambda: G.affine_select(out=r3(p[:], 4, 128), in_=r3(p[:], 4, 128),
                                                     compare_op=ALU.is_ge, fill=0.0, base=0,
                                                     pattern=[[0, 4], [1, 128]], channel_multiplier=-1), e)
        else:
            R["p", n] = R["evac", n] = dve(lambda: V.tensor_tensor(
                r3(p[:], 4, 128), r3(ps[bank][:], 4, 128), cmask.unsqueeze(1).to_broadcast([128, 4, 128]), ALU.mult),
                R["sc", b], R.get(("avn", n - 6)), e_rep, e_st, e_c)

    def cross(b):
        R["cross", b] = pe(lambda: mm(ps[6][:, 128:256], smt[:], qr[b % 2][:, 128:256], True, False), R["smt", b],
                           R.get(("rt", b - 1)), R.get("psd"))

    def av(b, c):
        for m in range(4):
            for g in range(4):
                n = 8 * b + 4 * c + g
                e = pe(lambda m=m, g=g, n=n: mm(ps[6][32 * g:32 * g + 32, 128 * c:128 * c + 128],
                                                vm[c][:, 160 * g + 32 * m:160 * g + 32 * m + 32],
                                                pt[n % 6][:, 128 * m:128 * m + 128], c == 0 and m == 0, m == 3),
                       R["p", n], R["vm", b], R.get(("rt", b - 1)), R.get("psd"))
                R["avn", n] = R["av", b] = e

    def evac(b):
        R["rt"] = R["rt", b] = act(lambda: A.copy(rt[:], ps[6][:, 0:256]), R["av", b], R.get(("cen", b - 1)))

    def centre(b):
        for c in range(2):
            e = pe(lambda c=c: mm(ps[7][:, 128 * c:128 * c + 128], rt[:, 128 * c:128 * c + 128], ccen),
                   R["rt", b], R.get(("base", b - 1)))
        R["cen", b] = e
        e = act(lambda: A.activation(sq[:], ps[7][:, 0:256], ACT.Square), e, R.get(("y", b - 1)))
        e = dve(lambda: V.tensor_reduce(vr[:], r3(sq[:], 32, 8), AX.X, ALU.add), e, R.get(("rn", b - 1)))
        R["sd", b] = act(lambda: A.activation(vr[:], vr[:], ACT.Sqrt, bias=eps[:], scale=0.125), e)

    def norm(b):
        e = dve(lambda: V.reciprocal(vr[:], vr[:]), R["sd", b])
        R["rn", b] = dve(lambda: V.tensor_tensor(r3(rn[:], 32, 8), r3(ps[7][:, 0:256], 32, 8),
                                                 vr[:].unsqueeze(2).to_broadcast([128, 32, 8]), ALU.mult), e,
                         R.get(("back", b - 1)))

    def back(b):
        for c in range(2):
            R["back", b] = pe(lambda c=c: T.transpose(ps[7][:, 256 + 128 * c:384 + 128 * c],
                                                      rn[:, 128 * c:128 * c + 128], ident[:]),
                              R["rn", b], R.get(("an", b - 1)))
        R["an", b] = act(lambda: A.activation(sq[:], ps[7][:, 256:512], ACT.Identity, bias=gbt[:, 1:2],
                                              scale=gbt[:, 0:1]), R["back", b])

    def load_x(b):
        R["xr", b] = sp.dma(lambda: nc.sync.dma_start(xr[b % 2][:].rearrange("p (c d) -> p c d", c=2), xrv[b]),
                            d_xr[b % 2], R.get(("base", b - 2)))

    def wout(b):
        for c in range(2):
            R["y", b] = pe(lambda c=c: mm(ps[7][:, 128 * c:128 * c + 128], sq[:, 128 * c:128 * c + 128],
                                          wv[:, 128:256]), R["an", b])
        R["base", b] = dve(lambda: V.tensor_tensor(ob[:], ps[7][:, 0:256], xr[b % 2][:], ALU.add), R["y", b], R["xr", b],
                           R.get(("ost", b - 1)))
        if b + 2 < NB:
            load_x(b + 2)
        R["ost", b] = sp.dma(lambda: nc.sync.dma_start(ov[b], ob[:].rearrange("p (c d) -> p c d", c=2)),
                             d_ob, R["base", b])

    X = {}
    regs, vregs, ready = {}, {}, {}

    def gather(t, *needs):
        X["g", t] = pool.dma(lambda: nc.gpsimd.indirect_dma_start(
            xg[t % 4][:], None, xnd, bass.IndirectOffsetOnAxis(ap=gidx[:, t:t + 1], axis=0)),
            d_g[t % 4], X.get(("xT", t - 4)), state["e"], e_st, *needs)

    def xtrans(t, *needs):
        X["xT", t] = pe(lambda: T.transpose(ps[5][:, 0:128], xg[t % 4][:], ident[:]), X["g", t], X.get(("x", t - 1)), *needs)
        X["x", t] = act(lambda: A.copy(xf[t % 2][:], ps[5][:, 0:128]), X["xT", t], X.get(("L1", t - 2)))

    def loadreg(t):
        regs[t] = nc.tensor.value_load(exi[0:1, t:t + 1], min_val=0, max_val=7)

    def fetch(t, *needs):
        def copy():
            vregs[t] = nc.vector.value_load(exi[0:1, t:t + 1], min_val=0, max_val=7)
            return V.tensor_copy(w1c[:], w1s[:, bass.ds(vregs[t] * 512, 512)])
        X["w1", t] = dve(copy, X.get(("L1", t - 1)), ready["w1"], state["e"], *needs)

    def layer1(t, *needs):
        def piece(c):
            if c == 0 and t < 2:
                loadreg(t)
            return mm(ps[0][:, 128 * c:128 * c + 128], w1c[:, 128 * c:128 * c + 128], xf[t % 2][:])
        for c in range(4):
            X["L1", t] = pe(lambda c=c: piece(c), X["x", t], X.get(("b1", t - 1)), X["w1", t])

    def bias1(t, *needs):
        X["b1", t] = dve(lambda: V.tensor_tensor(
            r3(g1[:], 4, 128), r3(ps[0][:], 4, 128),
            b1s[:, bass.ds(vregs[t] * 4, 4)].unsqueeze(2).to_broadcast([128, 4, 128]), ALU.add),
            X["L1", t], X.get(("h1l", t - 1)), e_b, *needs)
        if t + 1 < NT:
            fetch(t + 1)

    def gelu1(t):
        X["g1", t] = act(lambda: A.activation(g1[:], g1[:], ACT.Gelu), X["b1", t])

    def high(t):
        X["h1h", t] = act(lambda: A.copy(h1h[:], g1[:]), X["g1", t], X.get(("L2", t - 1)))

    def low(t):
        X["h1l", t] = dve(lambda: V.tensor_tensor(h1l[:], g1[:], h1h[:], ALU.subtract), X["h1h", t], X.get(("L2", t - 1)))

    stats(0)
    stats(1)
    e_rep = [rep_groups((0, 1), pool, lambda o_, i_, m: G.tensor_scalar(o_, i_, m, None, ALU.mult)),
             rep_groups((2, 3), act, lambda o_, i_, m: A.activation(o_, i_, ACT.Identity, scale=m))]
    normalise(0)
    transpose_x(0)
    proj(0, 1)
    stats(2)
    normalise(1)
    transpose_x(1)
    rotate(0, 1)
    proj(0, 0)
    expert_scores(0)
    stats(3)
    rotate(0, 0)
    expert_scores(1)
    normalise(2)
    normalise(3)
    e_st = sp.dma(lambda: nc.sync.dma_start(xnd.rearrange("(t p) d -> p t d", p=128), xv), d_xn, *e_xn)
    load_x(0)
    load_x(1)
    for i in range(4):
        load(i)
    stack(0, 1)
    unstack_k(0)
    transpose_x(2)
    transpose_x(3)
    stack(0, 0)
    expert_scores(2)
    unstack_q(0, 0)
    unstack_q(0, 1)
    projv(0)
    e_sc = expert_scores(3)
    unpackv(0)
    next(disp)
    e_cb = dve(lambda: V.tensor_copy(cbs[:], tmp2[:]), e_c)
    for b in range(NB):
        more = b + 1 < NB
        if b == NB - 2:
            gather(0)
        score(b, 0)
        if more:
            proj(b + 1, 1)
        score(b, 1)
        if more:
            rotate(b + 1, 1)
        if b < 6:
            next(disp)
        if b:
            centre(b - 1)
        ktrans(b)
        score(b, 2)
        if more:
            proj(b + 1, 0)
        score(b, 3)
        if more:
            rotate(b + 1, 0)
        smat(b)
        if b:
            norm(b - 1)
        if not more:
            gather(1, R["smt", b])
            for i in (20, 21):
                high_part(i, R["v", b], state["e"])
        if more:
            stage(2, 1)
        score(b, 4)
        next(disp, None)
        av(b, 0)
        if more:
            stack(b + 1, 1)
            unstack_k(b + 1)
        else:
            xtrans(0, R["qx", 1, b])
            fetch(0, R["kt", b], *R["qx", 0, b])
            for i in (22, 23):
                high_part(i, R["v", b], state["e"])
        score(b, 5)
        next(disp, None)
        if more:
            stage(1, 1)
        if b:
            back(b - 1)
        score(b, 6)
        if not more:
            layer1(0)
            bias1(0, R["kt", b], R["s", b])
        if more:
            stack(b + 1, 0)
        score(b, 7)
        if more:
            stage(0, 1)
        next(disp, None)
        if more:
            unstack_q(b + 1, 0)
            unstack_q(b + 1, 1)
            projv(b + 1)
        if b == NB - 2:
            ready["w1"] = load1(slice(8 - LATE, 8), R["rep", 0, b + 1], R["rot", 0, b + 1])
            e_b2 = act.dma(lambda: nc.scalar.dma_start(b2s[:], b23[:, 0:4096].partition_broadcast(128)), d_b2,
                           R["rep", 0, b + 1], R["rot", 0, b + 1])
        if not more:
            load_raw(R["sc", b])
            low_part(20, R["sc", b])
            gather(3, R["p", 8 * b + 6])
        if b:
            wout(b - 1)
        if not more:
            low_part(21)
        cross(b)
        av(b, 1)
        if not more:
            e_w3b = load3(slice(8 - LATE, 8), R["av", b], R["cross", b], R["s", b])
        evac(b)
        if more:
            unpackv(b + 1)
        if b == 0:
            load1(slice(0, 8 - LATE), R["gt"])
            load3(slice(0, 8 - LATE))
    assert next(disp, None) is None

    def layer2(t):
        bank = ps[2]

        def rhs(w, c):
            return w[:, bass.ds(regs[t] * 2048 + 512 * c, 512)]
        for c in range(4):
            cc = slice(128 * c, 128 * c + 128)
            pe(lambda c=c, cc=cc: mm(bank[:], h1h[:, cc], rhs(w2l, c), c == 0, False), X["h1l", t],
               X.get(("b2", t - 1)), *ready["w2"], sig=False)
            pe(lambda c=c, cc=cc: mm(bank[:], h1l[:, cc], rhs(w2h, c), False, False), sig=False)
            X["L2", t] = pe(lambda c=c, cc=cc: mm(bank[:], h1h[:, cc], rhs(w2h, c), False, c == 3))
            if c == 1 and t + 2 < NT:
                pe(lambda: loadreg(t + 2), sig=False)
        if t + 1 < NT:
            high(t + 1)
        X["b2", t] = dve(lambda: V.tensor_tensor(g2[:], bank[:], b2s[:, bass.ds(vregs[t] * 512, 512)], ALU.add),
                         X["L2", t], X.get(("T2", t - 1)), *ready["end"])
        X["g2", t] = act(lambda: A.activation(g2[:], g2[:], ACT.Gelu), X["b2", t])
        if t + 1 < NT:
            low(t + 1)

    def trans2(t):
        for c in range(4):
            X["T2", t] = pe(lambda c=c: T.transpose(ps[3][:, 128 * c:128 * c + 128], g2[:, 128 * c:128 * c + 128],
                                                    ident[:]), X["g2", t], X.get(("h2", t - 1)))
        X["h2", t] = act(lambda: A.copy(h2t[t % 2][:], ps[3][:]), X["T2", t], X.get(("L3", t - 2)))

    def layer3(t):
        bank = ps[4][:, 0:128]

        def rhs(c):
            return w3s[:, bass.ds(regs[t] * 512 + 128 * c, 128)]
        for c in range(4):
            X["L3", t] = pe(lambda c=c: mm(bank, h2t[t % 2][:, 128 * c:128 * c + 128], rhs(c), c == 0, c == 3),
                            X["h2", t], X.get(("ys", t - 1)), e_w3b)
        X["ys", t] = dve(lambda: V.scalar_tensor_tensor(ys[t % 2][:], bank, 0.5, b3s[:, bass.ds(vregs[t] * 128, 128)],
                                                        ALU.mult, ALU.add), X["L3", t], X.get(("add", t - 2)), e_b3)

    def scatter(t):
        X["add", t] = pool.dma(lambda: nc.gpsimd.indirect_dma_start(
            out, bass.IndirectOffsetOnAxis(ap=sidx[:, t:t + 1], axis=0), ys[t % 2][:], None,
            bounds_check=NTOK - 1, oob_is_err=False, compute_op=ALU.add),
            d_s, X["ys", t], X.get(("add", t - 1)), R["ost", NB - 1])

    centre(NB - 1)
    gather(2, R["cen", NB - 1])
    xtrans(1)
    low_part(22)
    layer1(1)
    after = [R["av", NB - 1], R["v", NB - 1]]
    on_pool = (pool, G.tensor_copy), (pool, G.tensor_tensor)
    for i in (25, 28):
        high_part(i, *after, on=on_pool[0])
        low_part(i, on=on_pool[1])
    high_part(24, *after)
    norm(NB - 1)
    gelu1(0)
    low_part(23)
    high(0)
    back(NB - 1)
    low_part(24)
    low(0)
    bias1(1)
    high_part(26, *after)
    low_part(26)
    wout(NB - 1)
    high_part(27, *after)
    low_part(27)
    high_part(29, *after)
    low_part(29, on=on_pool[1])
    gelu1(1)
    for i in (30, 31):
        high_part(i, *after)
        low_part(i)
    xtrans(2)
    ready["w2"] = list(lows.values())
    ready["end"] = [e_b2, R["ost", NB - 1], R["base", NB - 1], R["y", NB - 1]]
    for t in range(NT):
        if t + 4 < NT:
            gather(t + 4)
        if t == 0:
            e_b3 = halve_bias()
        layer2(t)
        if t + 3 < NT:
            xtrans(t + 3)
        if t:
            layer3(t - 1)
            scatter(t - 1)
        if t + 2 < NT:
            layer1(t + 2)
            bias1(t + 2)
            gelu1(t + 2)
        trans2(t)
    layer3(NT - 1)
    scatter(NT - 1)
    pool.ops.append((lambda: None, [X["add", NT - 1]], False))

    with nc.Block() as block:
        @block.sync
        def _(eng):
            sp.emit(eng)

        @block.scalar
        def _(eng):
            act.emit(eng)

        @block.vector
        def _(eng):
            dve.emit(eng)

        @block.gpsimd
        def _(eng):
            pool.emit(eng)

        @block.tensor
        def _(eng):
            pe.emit(eng)


def kernel(**inputs):
    import concourse.bacc as bacc
    from concourse.bass_utils import run_bass_kernel_spmd

    a = {k: np.asarray(v) for k, v in inputs.items()}
    swap = np.arange(128) ^ 1
    wqT = a["L0_attn_WQ"].reshape(128, 128).T
    wkT = a["L0_attn_WK"].reshape(128, 128).T
    wvT = a["L0_attn_WV"].reshape(128, 128).T
    cf, cb = constants()
    arrays = {
        "x": a["L0_attn_x"].reshape(NTOK, D),
        "wqkv": np.concatenate([wqT, wqT[:, swap], wkT, wkT[:, swap]], axis=1),
        "wvo": np.concatenate([wvT, a["L0_attn_WO"]], axis=1),
        "gb": np.stack([a["L0_attn_gamma"], a["L0_attn_beta"]], axis=1),
        "etokT": a["L0_ffn_expert_tokens"].T,
        "w1": a["L0_ffn_W1"], "w2": a["L0_ffn_W2"], "w3": a["L0_ffn_W3"],
        "b1t": a["L0_ffn_b1"].reshape(8, 4, 128).transpose(2, 0, 1).reshape(128, 32),
        "b23": np.concatenate([a["L0_ffn_b2"].reshape(1, 4096), a["L0_ffn_b3"].reshape(1, 1024)], axis=1),
        "cf": cf, "cb": cb,
    }
    arrays = {k: np.ascontiguousarray(v) for k, v in arrays.items()}
    nc = bacc.Bacc("TRN2", target_bir_lowering=False, num_devices=1)
    aps = {k: nc.dram_tensor(f"in_{k}", v.shape, mybir.dt.from_np(v.dtype), kind="ExternalInput").ap()
           for k, v in arrays.items()}
    out = nc.dram_tensor("out_0", (NTOK, D), F32, kind="ExternalOutput").ap()
    moe_retention_kernel(nc, *aps.values(), out)
    r = run_bass_kernel_spmd(nc, [{f"in_{k}": v for k, v in arrays.items()}], core_ids=[0])
    return r.results[0]["out_0"].reshape(8, 256, 128)
```
